# Optimizing a Trainium2 kernel written in Bass

```python
import numpy as np
import jax
import jax.numpy as jnp

def _softmax(x, axis=-1):
    return jax.nn.softmax(x, axis=axis)
def _gelu(x):
    return jax.nn.gelu(x, approximate=True)
def _silu(x):
    return jax.nn.silu(x)
def _sigmoid(x):
    return jax.nn.sigmoid(x)
def _layernorm(x, axis=-1, eps=1e-5):
    m = jnp.mean(x, axis=axis, keepdims=True)
    v = jnp.var(x, axis=axis, keepdims=True)
    return (x - m) / jnp.sqrt(v + eps)
def _scatter_add(tgt, idx, src, axis=0):
    return tgt.at[idx].add(src)
def _segment_sum(src, seg, n):
    return jax.ops.segment_sum(src, seg, n)

kernel_name = 'mk_conv_preact_d2_conv_nchw64_6a3e99'

def setup_inputs(seed: int = 0):
    np.random.seed(seed)
    _w = jnp.asarray
    def _rec_inputs():
        import jax
        import jax.numpy as jnp
        _gk = jax.random.key(seed)
        x = -0.000125 + 0.9999 * jax.random.normal(jax.random.fold_in(_gk, 1), (32, 64, 128, 128), jnp.float32)
        return x
    x = _rec_inputs()
    def _L0_conv_setup():
        import jax, jax.numpy as jnp
        import numpy as np
        from jax import lax
        B, CIN, H, W = (32, 64, 128, 128)
        COUT, K = (64, 3)
        STRIDE, PADDING = (1, 1)

        def _ste_binarize(v):
            clipped = jnp.clip(v, -1.0, 1.0)
            return lax.stop_gradient(jnp.sign(v) - clipped) + clipped
        key = jax.random.key(seed)
        kx, kw = jax.random.split(key)
        x = jax.random.normal(kx, (B, CIN, H, W), dtype=jnp.float32)
        weight = jax.random.uniform(kw, (COUT, CIN, K, K), dtype=jnp.float32) * 0.001
        return {'x': x, 'weight': weight}
    _L0_conv_all = _L0_conv_setup()
    _L0_conv_in = {k: v for k, v in _L0_conv_all.items() if k in ('weight', )}
    del _L0_conv_all

    def _L1_conv_setup():
        import jax, jax.numpy as jnp
        import numpy as np
        key = jax.random.key(seed)
        k0, k1, k2, k3 = jax.random.split(key, 4)
        B, dim, H, W = (8, 64, 256, 256)
        hidden = int(dim * 2.0)
        c2 = hidden * 2
        ps = 8
        x = jax.random.normal(k0, (B, dim, H, W), jnp.float32)
        w_in = jax.random.normal(k1, (c2, dim), jnp.float32) * 0.05
        w_dw = jax.random.normal(k2, (c2, 1, 3, 3), jnp.float32) * 0.05
        fft_params = jnp.ones((c2, 1, 1, ps, ps // 2 + 1), jnp.float32)
        w_out = jax.random.normal(k3, (dim, hidden), jnp.float32) * 0.05
        return {'x': x, 'w_in': w_in, 'w_dw': w_dw, 'fft_params': fft_params, 'w_out': w_out}
    _L1_conv_all = _L1_conv_setup()
    _L1_conv_in = {k: v for k, v in _L1_conv_all.items() if k in ('w_in', 'w_dw', 'fft_params', 'w_out', )}
    del _L1_conv_all

    return {
        "x": x,
        "L0_conv_weight": _L0_conv_in["weight"],
        "L1_conv_w_in": _L1_conv_in["w_in"],
        "L1_conv_w_dw": _L1_conv_in["w_dw"],
        "L1_conv_fft_params": _L1_conv_in["fft_params"],
        "L1_conv_w_out": _L1_conv_in["w_out"],
    }

def reference(x, L0_conv_weight, L1_conv_w_in, L1_conv_w_dw, L1_conv_fft_params, L1_conv_w_out):
    import jax
    import jax.numpy as jnp
    def _L0_conv_ref(x, weight):
        import jax, jax.numpy as jnp
        import numpy as np
        from jax import lax
        B, CIN, H, W = (32, 64, 128, 128)
        COUT, K = (64, 3)
        STRIDE, PADDING = (1, 1)

        def _ste_binarize(v):
            clipped = jnp.clip(v, -1.0, 1.0)
            return lax.stop_gradient(jnp.sign(v) - clipped) + clipped
        bx = _ste_binarize(x)
        bw = _ste_binarize(weight)
        y = lax.conv_general_dilated(bx, bw, window_strides=(STRIDE, STRIDE), padding=[(PADDING, PADDING), (PADDING, PADDING)], dimension_numbers=('NCHW', 'OIHW', 'NCHW'))
        return y

    def _L1_conv_ref(x, w_in, w_dw, fft_params, w_out):
        import jax, jax.numpy as jnp
        import numpy as np
        ps = 8
        h = jnp.einsum('oc,bchw->bohw', w_in, x)
        B, C, H, W = h.shape
        hp = h.reshape(B, C, H // ps, W // ps, ps, ps)
        hf = jnp.fft.rfft2(hp)
        hf = hf * jax.lax.stop_gradient(fft_params)
        hp = jnp.fft.irfft2(hf, s=(ps, ps)).astype(jnp.float32)
        h = hp.reshape(B, C, H, W)
        h = jax.lax.conv_general_dilated(h, w_dw, window_strides=(1, 1), padding='SAME', dimension_numbers=('NCHW', 'OIHW', 'NCHW'), feature_group_count=C)
        x1, x2 = jnp.split(h, 2, axis=1)
        g = jax.nn.gelu(x1, approximate=False) * x2
        return jnp.einsum('oc,bchw->bohw', w_out, g)

    def _gn(v, G=32, eps=1e-5):
        B_, C_, H_, W_ = v.shape
        g = v.reshape(B_, G, C_ // G, H_, W_)
        m = jnp.mean(g, axis=(2, 3, 4), keepdims=True)
        s = jnp.var(g, axis=(2, 3, 4), keepdims=True)
        return ((g - m) / jnp.sqrt(s + eps)).reshape(v.shape)

    def _ln_c(v, eps=1e-6):
        m = jnp.mean(v, axis=1, keepdims=True)
        s = jnp.var(v, axis=1, keepdims=True)
        return (v - m) / jnp.sqrt(s + eps)

    def _ln_t(v, eps=1e-5):
        m = jnp.mean(v, axis=-1, keepdims=True)
        s = jnp.var(v, axis=-1, keepdims=True)
        return (v - m) / jnp.sqrt(s + eps)

    def _to_tokens(v):
        B_, C_, H_, W_ = v.shape
        return v.reshape(B_, C_, H_ * W_).transpose(0, 2, 1)
    def _from_tokens(t, like):
        B_, C_, H_, W_ = like.shape
        return t.transpose(0, 2, 1).reshape(B_, C_, H_, W_)

    x = x + _L0_conv_ref(_gn(x), L0_conv_weight)
    x = x + _L1_conv_ref(_gn(x), L1_conv_w_in, L1_conv_w_dw, L1_conv_fft_params, L1_conv_w_out)
    return x


_drawn_inputs = setup_inputs


def setup_inputs(seed=0):
    import zlib

    import numpy as np

    out = dict(_drawn_inputs(seed))
    spreads = {'L1_conv_fft_params': (1.0, 0.6)}
    factors = {'L1_conv_w_in': 8.0, 'L1_conv_w_dw': 8.0, 'L1_conv_w_out': 8.0}
    for name, (base, spread) in spreads.items():
        noise = np.random.default_rng([zlib.crc32(name.encode()), seed]).standard_normal(out[name].shape)
        drawn = base * np.exp(spread * noise) if base else spread * noise
        out[name] = jnp.asarray(drawn.astype(out[name].dtype))
    for name, factor in factors.items():
        out[name] = (out[name] * factor).astype(out[name].dtype)
    return out
```

```python
from contextlib import ExitStack

import concourse.bass as bass
from concourse import mybir

F32 = mybir.dt.float32
BF16 = mybir.dt.bfloat16
ALU = mybir.AluOpType
ACT = mybir.ActivationFunctionType

B, C, H, W = 32, 64, 128, 128
HID = 128
PS = 8
STRIPS = H // PS
STEPS = STRIPS // 2
CHUNK = PS * W
TILES = PS
TAPS = 9
PE_TAPS = (3, 2)
RING = 4
EPS = 1e-5

STAT_FROM, CONV_FROM, STEP_FROM, LOAD_FROM = 14, 6, 14, 13
MEAN_SLOT, SPREAD_SLOT = 5, 13


def side_work(b, j):
    out = []
    if j >= STEP_FROM:
        out.append(("step", b + 1, j - STEP_FROM))
        out.append(("stat", b + 2, j - STAT_FROM))
    if j < STEP_FROM - STEPS:
        out.append(("step", b, j + 16 - STEP_FROM))
        out.append(("stat", b + 1, j + 16 - STAT_FROM))
    if CONV_FROM <= j < CONV_FROM + STEPS:
        out.append(("conv", b + 1, j - CONV_FROM))
    if CONV_FROM <= j + 1 < CONV_FROM + STEPS:
        out.append(("sign", b + 1, j + 1 - CONV_FROM))
    if j == MEAN_SLOT:
        out.append(("mean", b + 1, 0))
    if j == SPREAD_SLOT:
        out.append(("spread", b + 1, 0))
    return [w for w in out if 0 <= w[1] < B]


def bank_uses():
    number, n = {}, 0
    for b in range(-1, B + 1):
        for j in range(STRIPS):
            kinds = [k for k, _, _ in side_work(b, j)]
            project = 4 <= b * STRIPS + j < B * STRIPS + 4
            for name, there in (("P0", project), ("T0", "step" in kinds), ("C0", "conv" in kinds),
                                ("T1", "step" in kinds), ("P1", project), ("D0", "step" in kinds),
                                ("C1", "conv" in kinds), ("D1", "step" in kinds), ("M", "mean" in kinds),
                                ("S0", "spread" in kinds), ("S1", "spread" in kinds)):
                if there:
                    n += 1
                    number[b, j, name] = n
    return number


USES = bank_uses()
USES_PER_IMAGE = USES[2, 0, "P0"] - USES[1, 0, "P0"]


class Image:

    def __init__(self, v, like):
        self.v, self.like = v, like

    def count(self, per_image, more, d=0):
        return self.v * per_image + (per_image * d + more)

    def use(self, j, name):
        b, j = (self.like, j) if j >= 0 else (self.like - 1, j + STRIPS)
        return (self.v - self.like) * USES_PER_IMAGE + USES[b, j, name]

    def strip(self, j):
        return self.v * STRIPS + j

    def has(self, j):
        return 0 <= self.like * STRIPS + j < B * STRIPS


def reached(value):
    return max(value, 0) if isinstance(value, int) else value


def over_images(eng, slot, before=None):
    for j in range(STRIPS):
        slot(Image(-1, -1), j)
    if before:
        before()
    for j in range(STRIPS):
        slot(Image(0, 0), j)
    with eng.Fori(0, (B - 4) // 2) as i:
        for parity in (1, 2):
            for j in range(STRIPS):
                slot(Image(i * 2 + parity, parity), j)
    for b in range(B - 3, B):
        for j in range(STRIPS):
            slot(Image(b, b), j)
    for j in range(4):
        slot(Image(B, B), j)


def preact_layers(nc, x, w0, w_in, w_dw, fft, w_out, square, pick, out):
    ctx = ExitStack()
    with ctx:
        def sb(name, shape, dt=F32):
            return ctx.enter_context(nc.sbuf_tensor(name, shape, dt))

        def sem(name):
            return ctx.enter_context(nc.semaphore(name))

        X = [sb(f"X{i}", [128, H // 2, W]) for i in range(2)]
        spectra = sb("spectra", [128, STEPS, TILES, 128])
        signs = sb("signs", [128, H // 2 + 2, W + 2], BF16)
        copied_h = sb("copied_h", [128, 2, 2, 2 * HID])
        filtered = sb("filtered", [128, 2, TILES, 2 * HID])
        plane = sb("plane", [128, RING, 2, PS + 2, W + 2])
        gate = sb("gate", [128, 2, CHUNK])
        normed = sb("normed", [128, TILES, 128])
        turned = sb("turned", [128, TILES, 128])
        zeros = sb("zeros", [128, 2, W])
        sq = sb("sq", [128, 4, 128])
        ident, average, to_spectrum, to_pixels = (sq[:, i, :] for i in range(4))
        gains = sb("gains", [128, 2 * HID])
        diagonals = sb("diagonals", [128, 2, max(PE_TAPS), 128])
        w_in_sb = sb("w_in_sb", [128, 2 * HID])
        w_dw_sb = sb("w_dw_sb", [128, 2, TAPS])
        w_out_sb = sb("w_out_sb", [128, C])
        w_conv = sb("w_conv", [128, TAPS, 128], BF16)
        moments = sb("moments", [128, 2 * STEPS, 6])
        mean_var = sb("mean_var", [128, 2])
        neg_mean = sb("neg_mean", [128, 1])
        stat = sb("stat", [128, 8])
        power = sb("power", [128, 1])
        rstd = sb("rstd", [128, 1])
        w0_sb = X[1][:, 0:5, :].rearrange("p a b -> p (a b)")[:, 0:TAPS * C].rearrange("p (t c) -> p t c", t=TAPS)
        fft_sb = X[1][0:5 * PS, 8:10, :].rearrange("p a b -> p (a b)")
        pick_sb = X[1][0:5 * PS, 10, :]

        sums = [ctx.enter_context(nc.psum_tensor(f"sums{c}", [128, PS, W], F32)) for c in range(2)]
        mixed_h = [ctx.enter_context(nc.psum_tensor(f"mixed_h{i}", [128, 2, 256], F32)) for i in range(2)]
        fresh = ctx.enter_context(nc.psum_tensor("fresh", [128, 4, W], F32))
        side = ctx.enter_context(nc.psum_tensor("side", [128, 512], F32))

        weights_in = sem("weights_in")
        cleared = sem("cleared")
        signs_cleared = sem("signs_cleared")
        tables_raw = sem("tables_raw")
        tables = sem("tables")
        diagonals_done = sem("diagonals_done")
        conv_signs = sem("conv_signs")
        x_in = [sem(f"x_in{k}") for k in range(STEPS)]
        stored = [sem(f"stored{k}") for k in range(STEPS)]
        side_full = sem("side_full")
        side_free = sem("side_free")
        own_moments = sem("own_moments")
        own = sem("own")
        centred = sem("centred")
        signed = sem("signed")
        with_eps = sem("with_eps")
        rstd_done = sem("rstd_done")
        step_normed = sem("step_normed")
        mixed = sem("mixed")
        copied = sem("copied")
        framed = sem("framed")
        fresh_full = sem("fresh_full")
        kept = sem("kept")
        haloed = sem("haloed")
        started = sem("started")
        tapped = sem("tapped")
        gelu_done = sem("gelu_done")
        gated = sem("gated")

        block = ctx.enter_context(nc.Block())

        def normal_parts(img, j):
            return {k: (a - img.like, part) for k, a, part in side_work(img.like, j)}

        def taps_done(img, j, c, n=None):
            ops = [2 * (TAPS - p) for p in PE_TAPS]
            n = ops[c] if n is None else n
            return img.count(sum(ops) * STRIPS, sum(ops) * j + (ops[0] if c else 0) + n)

        def step_use(img, j):
            k = j % STEPS
            return img.use(k - (16 - STEP_FROM) if k >= 16 - STEP_FROM else k - 16 + STEP_FROM, "D1")

        @block.sync
        def _(sp):
            for dst, src in ((sq[:, :, :], square), (pick_sb, pick), (fft_sb, fft), (w_out_sb[:, :], w_out),
                             (w_dw_sb[:, :, :], w_dw.rearrange("(c p) t -> p c t", p=HID))):
                sp.dma_start(dst, src).then_inc(weights_in, 16)
            for h in range(2):
                sp.dma_start(w0_sb[64 * h:64 * h + 64], w0).then_inc(weights_in, 16)
                sp.dma_start(w_in_sb[64 * h:64 * h + 64, :], w_in).then_inc(weights_in, 16)

            def image_of(dram, img, d):
                first = 1 if img.like + d > 0 else 0
                part = dram[first:B][bass.ds(img.v + (d - first), 1)]
                return part.rearrange("a c (h r) w -> (a h) c (r w)", h=2)

            def load(img, d, k):
                sp.wait_ge(stored[k], reached(img.count(32, 0, d - 1)))
                for h in range(2):
                    src = image_of(x, img, d)
                    sp.dma_start(X[(img.like + d) % 2][64 * h:64 * h + 64, PS * k:PS * k + PS, :]
                                 .rearrange("p r w -> p (r w)"),
                                 src[h, :, k * CHUNK:(k + 1) * CHUNK]).then_inc(x_in[k], 16)

            for k in range(STEPS):
                load(Image(-1, -1), 1, k)

            def slot(img, j):
                if j >= LOAD_FROM and img.like + 2 < B:
                    if img.like == -1 and j == LOAD_FROM:
                        sp.wait_ge(tables_raw, 1)
                        sp.wait_ge(conv_signs, 2)
                        sp.wait_ge(own, 1)
                    load(img, 2, j - LOAD_FROM)
                if img.like >= 0 and j < STEPS - (STRIPS - LOAD_FROM) and img.like + 1 < B:
                    load(img, 1, j + STRIPS - LOAD_FROM)
                if img.has(j - 4):
                    s = (j - 4) % STRIPS
                    par = (img.like if j >= 4 else img.like - 1) % 2
                    h, k = s // STEPS, s % STEPS
                    sp.wait_ge(side_free, reached(img.use(j, "P1")))
                    dst = image_of(out, img, 0 if j >= 4 else -1)
                    sp.dma_start(dst[h, :, k * CHUNK:(k + 1) * CHUNK],
                                 X[par][64 * h:64 * h + 64, PS * k:PS * k + PS, :]
                                 .rearrange("p r w -> p (r w)")).then_inc(stored[k], 16)

            over_images(sp, slot)
            for k in range(STEPS):
                sp.wait_ge(stored[k], 32 * B)

        @block.gpsimd
        def _(pool):
            nc.gpsimd.memset(signs[:], 0.0).then_inc(signs_cleared, 1)
            nc.gpsimd.memset(power[:], -0.5).then_inc(signs_cleared, 1)
            nc.gpsimd.memset(zeros[:], 0.0).then_inc(signs_cleared, 1)

            def frame(img, j, u):
                m = img.count(4 * STRIPS, 4 * j + u)
                pool.wait_ge(copied, reached(m + 1))
                if u % 2 == 0:
                    pool.wait_ge(fresh_full, reached(img.count(4 * STRIPS, 4 * (j - 2) + 2 * (u // 2) + 2)))
                if img.like == 0 and j == 0 and u == 0:
                    pool.wait_ge(tables, 1)
                for i in range(2):
                    last = nc.gpsimd.tensor_tensor(filtered[:, j % 2, 2 * u + i, :], copied_h[:, u % 2, i, :],
                                                   gains[:, :], ALU.mult)
                last.then_inc(framed, 1)

            def halo(img, j):
                s, ring = j % STRIPS, j % RING
                pool.wait_ge(kept, reached(img.count(4 * STRIPS, 4 * j + 4)))
                pool.wait_ge(tapped, reached(taps_done(img, j - 3, 1)))
                def put(dst, row):
                    return nc.gpsimd.tensor_tensor(dst, row, zeros[:, :, :], ALU.subtract)

                if s > 0:
                    put(plane[:, (ring - 1) % RING, :, PS + 1, 1:W + 1], plane[:, ring, :, 1, 1:W + 1])
                if s == STRIPS - 1:
                    put(plane[:, ring, :, PS + 1, 1:W + 1], zeros[:, :, :])
                last_row = plane[:, ring, :, PS, 1:W + 1] if s < STRIPS - 1 else zeros[:, :, :]
                put(plane[:, (ring + 1) % RING, :, 0, 1:W + 1], last_row).then_inc(haloed, 1)

            def slot(img, j):
                if img.has(j):
                    frame(img, j, 0)
                    frame(img, j, 1)
                if img.has(j):
                    frame(img, j, 2)
                    frame(img, j, 3)
                if img.has(j - 1):
                    halo(img, j - 1)
                if "spread" in normal_parts(img, j):
                    d, _ = normal_parts(img, j)["spread"]
                    pool.wait_ge(with_eps, reached(img.count(1, 1, d)))
                    nc.gpsimd.tensor_tensor(rstd[:], stat[:, 3:4], power[:], ALU.pow).then_inc(rstd_done, 1)

            pool.wait_ge(signs_cleared, 3)
            over_images(pool, slot)

        @block.scalar
        def _(act):
            act.wait_ge(weights_in, 16 * 9)
            act.wait_ge(cleared, 2)
            for h in range(2):
                nc.scalar.activation(w_conv[64 * h:64 * h + 64, :, 64 * h:64 * h + 64], w0_sb[64 * h:64 * h + 64],
                                     ACT.Sign).then_inc(conv_signs, 1)

            def keep(use, dst):
                act.wait_ge(side_full, reached(use))
                nc.scalar.copy(dst, side[:, :].rearrange("p (t f) -> p t f", t=4)).then_inc(side_free, 1)

            def keep_pixels(img, j, q, c):
                act.wait_ge(fresh_full, reached(img.count(4 * STRIPS, 4 * j + 2 * q + c + 1)))
                act.wait_ge(tapped, reached(taps_done(img, j - RING, 1)))
                nc.scalar.copy(plane[:, j % RING, c, 1 + 4 * q:5 + 4 * q, 1:W + 1], fresh[:, :, :]).then_inc(kept, 1)

            def sign_part(img, d, k):
                Xa = X[(img.like + d) % 2]
                nc.scalar.activation(signs[:, 1 + PS * k:1 + PS * k + PS, 1:W + 1], Xa[:, PS * k:PS * k + PS, :],
                                     ACT.Sign, bias=neg_mean[:, 0:1]).then_inc(signed, 1)

            def slot(img, j):
                parts = normal_parts(img, j)
                for q in range(2):
                    if img.has(j - 1):
                        keep_pixels(img, j - 1, q, 0)
                        keep_pixels(img, j - 1, q, 1)
                    if img.has(j):
                        for u in (2 * q, 2 * q + 1):
                            m = img.count(4 * STRIPS, 4 * j + u)
                            act.wait_ge(mixed, reached(m + 1))
                            act.wait_ge(framed, reached(m - 1))
                            nc.scalar.copy(copied_h[:, u % 2], mixed_h[u % 2][:, :, :]).then_inc(copied, 1)
                    if q == 0 and img.has(j - 3):
                        act.wait_ge(tapped, reached(taps_done(img, j - 3, 0)))
                        if img.has(j - 5):
                            act.wait_ge(side_full, reached(img.use(j - 1, "P1")))
                        nc.scalar.activation(gate[:, (j - 3) % 2, :], sums[0][:, :, :].rearrange("p y x -> p (y x)"),
                                             ACT.Gelu).then_inc(gelu_done, 1)
                    if "step" in parts:
                        d, k = parts["step"]
                        for i in range(2):
                            if q == 0:
                                keep(img.use(j, f"T{i}"), turned[:, 4 * i:4 * i + 4, :])
                            else:
                                keep(img.use(j, f"D{i}"), spectra[:, k, 4 * i:4 * i + 4, :])

                if "sign" in parts:
                    d, k = parts["sign"]
                    if k == 0:
                        Xa = X[(img.like + d) % 2]
                        act.wait_ge(centred, reached(img.count(1, 1, d)))
                        if img.like == -1:
                            act.wait_ge(signs_cleared, 3)
                        sign_part(img, d, 0)
                        nc.scalar.activation(signs[64:128, 0, 1:W + 1], Xa[0:64, H // 2 - 1, :], ACT.Sign,
                                             bias=neg_mean[0:64, 0:1]).then_inc(signed, 1)
                        nc.scalar.activation(signs[0:64, H // 2 + 1, 1:W + 1], Xa[64:128, 0, :], ACT.Sign,
                                             bias=neg_mean[64:128, 0:1]).then_inc(signed, 1)
                    if k + 1 < STEPS:
                        sign_part(img, d, k + 1)

            over_images(act, slot)

        @block.tensor
        def _(pe):
            pe.wait_ge(weights_in, 16 * 9)
            nc.tensor.matmul(side[:, 0:256], pick_sb, fft_sb, start=True, stop=True).then_inc(tables_raw, 1)
            pe.wait_ge(conv_signs, 2)

            def mix(img, j, q):
                h, k = (j % STRIPS) // STEPS, j % STEPS
                after = j >= STRIPS
                if q == 0:
                    pe.wait_ge(side_free, reached(step_use(Image(img.v + 1, img.like + 1) if after else img, j % STRIPS)))
                for u in (2 * q, 2 * q + 1):
                    pe.wait_ge(copied, reached(img.count(4 * STRIPS, 4 * j + u - 1)))
                    for i in range(2):
                        last = nc.tensor.matmul(mixed_h[u % 2][:, i, :], spectra[64 * h:64 * h + 64, k, 2 * u + i, :],
                                                w_in_sb[64 * h:64 * h + 64, :], start=True, stop=True)
                    last.then_inc(mixed, 1)

            def pixels(img, j, q, c):
                pe.wait_ge(framed, reached(img.count(4 * STRIPS, 4 * j + 2 * q + 2)))
                pe.wait_ge(kept, reached(img.count(4 * STRIPS, 4 * j + 2 * q + c)))
                for t in range(4):
                    last = nc.tensor.matmul(fresh[:, t, :], filtered[:, j % 2, 4 * q + t, HID * c:HID * c + HID],
                                            to_pixels, start=True, stop=True)
                last.then_inc(fresh_full, 1)

            def start_taps(img, j, c):
                pe.wait_ge(haloed, reached(img.strip(j) + (1 if j % STRIPS == STRIPS - 1 else 2)))
                if c == 0:
                    pe.wait_ge(gelu_done, reached(img.strip(j)))
                else:
                    pe.wait_ge(gated, reached(img.strip(j)))
                for q in range(2):
                    for n in range(PE_TAPS[c]):
                        last = nc.tensor.matmul(sums[c][:, 4 * q:4 * q + 4, :], diagonals[:, c, n, :],
                                                plane[:, j % RING, c, 4 * q + n // 3:4 * q + n // 3 + 4, n % 3:n % 3 + W],
                                                start=(n == 0), stop=(n == PE_TAPS[c] - 1))
                last.then_inc(started, 1)

            def side_bank(use):
                pe.wait_ge(side_free, reached(use - 1))

            def project(img, j, q):
                s = (j - 4) % STRIPS
                h = s // STEPS
                side_bank(img.use(j, f"P{q}"))
                pe.wait_ge(gated, reached(img.strip(j - 3)))
                nc.tensor.matmul(side[64 * h:64 * h + 64, :], w_out_sb[:, :], gate[:, (j - 4) % 2, 512 * q:512 * q + 512],
                                 start=True, stop=True).then_inc(side_full, 1)

            def turn(img, j, d, k, i):
                side_bank(img.use(j, f"T{i}"))
                if i == 0:
                    pe.wait_ge(step_normed, reached(img.count(STEPS, k + 1, d)))
                for t in range(4):
                    last = nc.tensor.transpose(side[:, 128 * t:128 * t + 128], normed[:, 4 * i + t, :], ident)
                last.then_inc(side_full, 1)

            def spectrum(img, j, i):
                side_bank(img.use(j, f"D{i}"))
                pe.wait_ge(side_free, reached(img.use(j, f"T{i}")))
                for t in range(4):
                    last = nc.tensor.matmul(side[:, 128 * t:128 * t + 128], turned[:, 4 * i + t, :], to_spectrum,
                                            start=True, stop=True)
                last.then_inc(side_full, 1)

            def conv(img, j, d, k, i):
                side_bank(img.use(j, f"C{i}"))
                pe.wait_ge(signed, reached(img.count(STEPS + 2, min(k + 1, STEPS - 1) + 3, d)))
                row = PS * k + 4 * i
                for tap in range(TAPS):
                    dy, dx = tap // 3, tap % 3
                    last = nc.tensor.matmul(side[:, :], w_conv[:, tap, :], signs[:, row + dy:row + dy + 4, dx:dx + W],
                                            start=(tap == 0), stop=(tap == TAPS - 1))
                last.then_inc(side_full, 1)

            def group_mean(img, j, name, col, which, d):
                side_bank(img.use(j, name))
                pe.wait_ge(own_moments, reached(img.count(3, which, d)))
                nc.tensor.matmul(side[:, 0:1], average, col, start=True, stop=True).then_inc(side_full, 1)

            def slot(img, j):
                parts = normal_parts(img, j)
                if img.has(j - 3):
                    start_taps(img, j - 3, 1)
                if img.has(j - 4):
                    project(img, j, 0)
                if img.has(j - 1):
                    pixels(img, j - 1, 0, 0)
                if "step" in parts:
                    turn(img, j, *parts["step"], 0)
                if "conv" in parts:
                    conv(img, j, *parts["conv"], 0)
                if img.has(j - 1):
                    pixels(img, j - 1, 0, 1)
                if img.has(j):
                    mix(img, j, 1)
                if "step" in parts:
                    turn(img, j, *parts["step"], 1)
                if img.has(j - 1):
                    pixels(img, j - 1, 1, 0)
                if img.has(j - 4):
                    project(img, j, 1)
                if "step" in parts:
                    spectrum(img, j, 0)
                if "conv" in parts:
                    conv(img, j, *parts["conv"], 1)
                if img.has(j - 1):
                    pixels(img, j - 1, 1, 1)
                if img.has(j + 1) and img.like >= 0:
                    mix(img, j + 1, 0)
                if "step" in parts:
                    spectrum(img, j, 1)
                if img.has(j - 2):
                    start_taps(img, j - 2, 0)
                if "mean" in parts:
                    group_mean(img, j, "M", mean_var[:, 0:1], 1, parts["mean"][0])
                if "spread" in parts:
                    d = parts["spread"][0]
                    group_mean(img, j, "S0", mean_var[:, 0:1], 2, d)
                    group_mean(img, j, "S1", stat[:, 2:3], 3, d)

            over_images(pe, slot, before=lambda: (pe.wait_ge(tables, 1), pe.wait_ge(diagonals_done, sum(PE_TAPS)), mix(Image(0, 0), 0, 0)))

        @block.vector
        def _(dve):
            nc.vector.memset(w_conv[:], 0.0).then_inc(cleared, 1)
            nc.vector.memset(plane[:], 0.0).then_inc(cleared, 1)
            dve.wait_ge(weights_in, 16 * 9)
            for c in range(2):
                for n in range(PE_TAPS[c]):
                    nc.vector.tensor_scalar(diagonals[:, c, n, :], ident, w_dw_sb[:, c, n:n + 1], None,
                                            ALU.mult).then_inc(diagonals_done, 1)
            dve.wait_ge(tables_raw, 1)
            nc.vector.tensor_copy(gains[:, :], side[:, 0:256]).then_inc(tables, 1)

            def chunk_moments(Xa, k, i):
                return nc.vector.bn_stats(moments[:, 2 * k + i, :],
                                          Xa[:, PS * k + 4 * i:PS * k + 4 * i + 4, :].rearrange("p r w -> p (r w)"))

            def stat_part(img, d, k):
                dve.wait_ge(x_in[k], reached(img.count(32, 32, d)))
                for i in range(2):
                    last = chunk_moments(X[(img.like + d) % 2], k, i)
                if k == STEPS - 1:
                    last.then_inc(own, 1)

            def aggregate_after_wait():
                nc.vector.memset(stat[:, 6:7], 0.0)

            def mean_part(img, j, d):
                dve.wait_ge(own, reached(img.count(3, 1, d)))
                aggregate_after_wait()
                nc.vector.bn_aggr(mean_var[:, :], moments[:, :, :].rearrange("p n s -> p (n s)")).then_inc(own_moments, 1)
                dve.wait_ge(side_full, reached(img.use(j, "M")))
                nc.vector.tensor_scalar(neg_mean[:, :], side[:, 0:1], -1.0, None, ALU.mult).then_inc(centred, 1)
                dve.wait_ge(centred, reached(img.count(1, 1, d)))
                nc.vector.tensor_copy(stat[:, 4:5], side[:, 0:1]).then_inc(side_free, 1)

            def spread_part(img, j, d):
                dve.wait_ge(own, reached(img.count(3, 2, d)))
                aggregate_after_wait()
                nc.vector.bn_aggr(mean_var[:, :], moments[:, :, :].rearrange("p n s -> p (n s)")).then_inc(own_moments, 1)
                dve.wait_ge(side_full, reached(img.use(j, "S0")))
                dve.wait_ge(own_moments, reached(img.count(3, 2, d)))
                nc.vector.tensor_copy(stat[:, 0:1], side[:, 0:1]).then_inc(own, 1)
                nc.vector.tensor_tensor(stat[:, 1:2], side[:, 0:1], mean_var[:, 0:1], ALU.subtract).then_inc(side_free, 1)
                dve.wait_ge(side_free, reached(img.use(j, "S0")))
                nc.vector.scalar_tensor_tensor(out=stat[:, 2:3], in0=stat[:, 1:2], scalar=stat[:, 1:2],
                                               in1=mean_var[:, 1:2], op0=ALU.mult, op1=ALU.add).then_inc(own_moments, 1)
                dve.wait_ge(side_full, reached(img.use(j, "S1")))
                nc.vector.tensor_scalar(stat[:, 3:4], side[:, 0:1], EPS, None, ALU.add).then_inc(with_eps, 1)
                dve.wait_ge(with_eps, reached(img.count(1, 1, d)))
                nc.vector.tensor_copy(stat[:, 5:6], side[:, 0:1]).then_inc(side_free, 1)

            def normalise(img, j, d, k):
                dve.wait_ge(rstd_done, reached(img.count(1, 1, d)))
                dve.wait_ge(own, reached(img.count(3, 3, d)))
                if k > 0:
                    dve.wait_ge(side_full, reached(img.use(j - 1, "T1")))
                elif img.like + d > 0:
                    dve.wait_ge(side_full, reached(img.use(j - (STRIPS - STEPS) - 1, "T1")))
                nc.vector.tensor_scalar(normed[:, :, :], X[(img.like + d) % 2][:, PS * k:PS * k + PS, :],
                                        stat[:, 0:1], rstd[:, 0:1], ALU.subtract, ALU.mult).then_inc(step_normed, 1)

            def conv_part(img, j, d, k, i):
                dve.wait_ge(side_full, reached(img.use(j, f"C{i}")))
                rows = X[(img.like + d) % 2][:, PS * k + 4 * i:PS * k + 4 * i + 4, :].rearrange("p r w -> p (r w)")
                nc.vector.tensor_tensor(rows, side[:, :], rows, ALU.add).then_inc(side_free, 1)

            def conv_moments(img, j, d, k, i):
                dve.wait_ge(side_free, reached(img.use(j, f"C{i}")))
                last = chunk_moments(X[(img.like + d) % 2], k, i)
                if (k, i) == (STEPS - 1, 1):
                    last.then_inc(own, 1)

            def add_taps(img, j, c):
                dve.wait_ge(started, reached(img.count(2 * STRIPS, 2 * j + c + 1)))
                for n in range(2 * (TAPS - PE_TAPS[c])):
                    tap, q = PE_TAPS[c] + n // 2, n % 2
                    if n >= 2:
                        dve.wait_ge(tapped, reached(taps_done(img, j, c, n - 1)))
                    rows = sums[c][:, 4 * q:4 * q + 4, :]
                    nc.vector.scalar_tensor_tensor(
                        out=rows,
                        in0=plane[:, j % RING, c, 4 * q + tap // 3:4 * q + tap // 3 + 4, tap % 3:tap % 3 + W],
                        scalar=w_dw_sb[:, c, tap:tap + 1], in1=rows, op0=ALU.mult, op1=ALU.add).then_inc(tapped, 1)

            def gate_part(img, j):
                dve.wait_ge(gelu_done, reached(img.strip(j + 1)))
                dve.wait_ge(tapped, reached(taps_done(img, j, 1)))
                g = gate[:, j % 2, :]
                nc.vector.tensor_tensor(g, sums[1][:, :, :].rearrange("p y x -> p (y x)"), g, ALU.mult).then_inc(gated, 1)

            def residual(img, j, q):
                s = (j - 4) % STRIPS
                par = (img.like if j >= 4 else img.like - 1) % 2
                h, k = s // STEPS, s % STEPS
                dve.wait_ge(side_full, reached(img.use(j, f"P{q}")))
                px = X[par][64 * h:64 * h + 64, PS * k + 4 * q:PS * k + 4 * q + 4, :]
                nc.vector.tensor_tensor(px, side[64 * h:64 * h + 64, :].rearrange("p (y x) -> p y x", y=4), px,
                                        ALU.add).then_inc(side_free, 1)

            def slot(img, j):
                parts = normal_parts(img, j)
                if "step" in parts:
                    normalise(img, j, *parts["step"])
                for q in range(2):
                    if img.has(j - 3):
                        add_taps(img, j - 3, q)
                    if img.has(j - 4):
                        residual(img, j, q)
                    if q == 1 and img.has(j - 3):
                        gate_part(img, j - 3)
                    if "conv" in parts:
                        conv_part(img, j, *parts["conv"], q)
                        conv_moments(img, j, *parts["conv"], q)
                if "stat" in parts:
                    stat_part(img, *parts["stat"])
                if "mean" in parts:
                    mean_part(img, j, parts["mean"][0])
                if "spread" in parts:
                    spread_part(img, j, parts["spread"][0])

            for k in range(16 - STAT_FROM):
                stat_part(Image(-1, -1), 1, k)
            over_images(dve, slot)


def fourier_constants():
    import numpy as np
    y, x = np.meshgrid(np.arange(PS), np.arange(PS), indexing="ij")
    basis, pick = [], []
    for v in range(PS // 2 + 1):
        for u in range(PS):
            paired = v in (0, PS // 2)
            if paired and u > PS // 2:
                continue
            angle = 2 * np.pi * (u * y + v * x) / PS
            own = np.zeros((PS, PS // 2 + 1))
            if paired:
                own[u, v] += 0.5
                own[-u % PS, v] += 0.5
            else:
                own[u, v] = 1
            if paired and u in (0, PS // 2):
                members = [np.cos(angle) / PS]
            else:
                members = [f(angle) * np.sqrt(2) / PS for f in (np.cos, np.sin)]
            for q in members:
                basis.append(q.ravel())
                pick.append(own.ravel())
    basis, pick = np.stack(basis), np.stack(pick, 1)
    ident = np.eye(128)
    average = np.zeros((128, 128))
    for p in range(128):
        for o in range(128):
            if (p % C) // 2 == (o % C) // 2:
                average[p, o] = 0.25
    to_pixels = np.kron(np.eye(2), basis)
    square = np.stack([ident, average, to_pixels.T, to_pixels], 1)
    return {"square": square.astype(np.float32), "pick": np.concatenate([pick, pick], 1).astype(np.float32)}


def kernel(**inputs):
    import numpy as np
    import concourse.bacc as bacc
    from concourse.bass_utils import run_bass_kernel_spmd as run

    a = {k: np.asarray(v) for k, v in inputs.items()}
    arrays = {
        "x": a["x"],
        "w0": a["L0_conv_weight"].transpose(1, 2, 3, 0).reshape(C, TAPS, C),
        "w_in": a["L1_conv_w_in"].T,
        "w_dw": a["L1_conv_w_dw"].reshape(2 * HID, TAPS),
        "fft": a["L1_conv_fft_params"].reshape(2 * HID, 5 * PS).T,
        "w_out": a["L1_conv_w_out"].T,
    }
    arrays.update(fourier_constants())
    arrays = {k: np.ascontiguousarray(v) for k, v in arrays.items()}
    nc = bacc.Bacc("TRN2", target_bir_lowering=False, num_devices=1)
    args = [nc.dram_tensor(f"in_{k}", v.shape, mybir.dt.from_np(v.dtype), kind="ExternalInput").ap()
            for k, v in arrays.items()]
    out = nc.dram_tensor("result", a["x"].shape, F32, kind="ExternalOutput").ap()
    preact_layers(nc, *args, out)
    got = run(nc, [{f"in_{k}": v for k, v in arrays.items()}], core_ids=[0])
    return got.results[0]["result"]
```

```python
from contextlib import ExitStack

import concourse.bass as bass
from concourse import mybir

F32 = mybir.dt.float32
BF16 = mybir.dt.bfloat16
ALU = mybir.AluOpType
ACT = mybir.ActivationFunctionType

B, C, H, W = 32, 64, 128, 128
HID = 128
PS = 8
STRIPS = H // PS
STEPS = STRIPS // 2
CHUNK = PS * W
TILES = PS
TAPS = 9
PE_TAPS = (2, 2)
RING = 4
EPS = 1e-5

STAT_FROM, CONV_FROM, STEP_FROM, LOAD_FROM = 14, 6, 15, 13
MEAN_SLOT, SPREAD_SLOT = 5, 14


def side_work(b, j):
    out = []
    if j >= STEP_FROM:
        out.append(("step", b + 1, j - STEP_FROM))
    if j < STEP_FROM - STEPS:
        out.append(("step", b, j + STRIPS - STEP_FROM))
    if j >= STAT_FROM:
        out.append(("stat", b + 2, j - STAT_FROM))
    if j < STAT_FROM - STEPS:
        out.append(("stat", b + 1, j + STRIPS - STAT_FROM))
    if CONV_FROM <= j < CONV_FROM + STEPS:
        out.append(("conv", b + 1, j - CONV_FROM))
    if CONV_FROM <= j - 1 < CONV_FROM + STEPS:
        out.append(("late", b + 1, j - 1 - CONV_FROM))
    if CONV_FROM <= j + 1 < CONV_FROM + STEPS:
        out.append(("sign", b + 1, j + 1 - CONV_FROM))
    if j == MEAN_SLOT:
        out.append(("mean", b + 1, 0))
    if j == SPREAD_SLOT:
        out.append(("spread", b + 1, 0))
    return [w for w in out if 0 <= w[1] < B]


def bank_uses():
    number, n = {}, 0
    for b in range(-1, B + 1):
        for j in range(STRIPS):
            kinds = [k for k, _, _ in side_work(b, j)]
            project = 4 <= b * STRIPS + j < B * STRIPS + 4
            for name, there in (("T0", "step" in kinds), ("C0", "conv" in kinds), ("T1", "step" in kinds),
                                ("P0", project), ("M", "mean" in kinds), ("S0", "spread" in kinds),
                                ("S1", "spread" in kinds), ("D0", "step" in kinds), ("P1", project),
                                ("D1", "step" in kinds), ("C1", "conv" in kinds)):
                if there:
                    n += 1
                    number[b, j, name] = n
    return number


USES = bank_uses()
USES_PER_IMAGE = USES[2, 0, "P0"] - USES[1, 0, "P0"]


class Image:

    def __init__(self, v, like):
        self.v, self.like = v, like

    def count(self, per_image, more, d=0):
        return self.v * per_image + (per_image * d + more)

    def use(self, j, name):
        b, j = (self.like, j) if j >= 0 else (self.like - 1, j + STRIPS)
        return (self.v - self.like) * USES_PER_IMAGE + USES[b, j, name]

    def strip(self, j):
        return self.v * STRIPS + j

    def has(self, j):
        return 0 <= self.like * STRIPS + j < B * STRIPS


def reached(value):
    return max(value, 0) if isinstance(value, int) else value


def over_images(eng, slot, before=None):
    for j in range(STRIPS):
        slot(Image(-1, -1), j)
    if before:
        before()
    for j in range(STRIPS):
        slot(Image(0, 0), j)
    with eng.Fori(0, (B - 4) // 2) as i:
        for parity in (1, 2):
            for j in range(STRIPS):
                slot(Image(i * 2 + parity, parity), j)
    for b in range(B - 3, B):
        for j in range(STRIPS):
            slot(Image(b, b), j)
    for j in range(4):
        slot(Image(B, B), j)


def preact_layers(nc, x, w0, w_in, w_dw, fft, w_out, square, pick, out):
    ctx = ExitStack()
    with ctx:
        def sb(name, shape, dt=F32):
            return ctx.enter_context(nc.sbuf_tensor(name, shape, dt))

        def sem(name):
            return ctx.enter_context(nc.semaphore(name))

        X = [sb(f"X{i}", [128, H // 2, W]) for i in range(2)]
        spectra = sb("spectra", [128, STEPS, TILES, 128])
        signs = sb("signs", [128, H // 2 + 2, W + 2], BF16)
        copied_h = sb("copied_h", [128, 2, 2, 2 * HID])
        filtered = sb("filtered", [128, 2, TILES, 2 * HID])
        plane = sb("plane", [128, RING, 2, PS + 2, W + 2])
        gate = sb("gate", [128, 2, CHUNK])
        second = sb("second", [128, CHUNK])
        from_side = sb("from_side", [128, 512])
        projected = sb("projected", [128, 512])
        normed = sb("normed", [128, TILES, 128])
        turned = sb("turned", [128, TILES, 128])
        zeros = sb("zeros", [128, 1, 1])
        sq = sb("sq", [128, 4, 128])
        ident, average, to_spectrum, to_pixels = (sq[:, i, :] for i in range(4))
        gains = sb("gains", [128, 2 * HID])
        diagonals = sb("diagonals", [128, 2, max(PE_TAPS), 128])
        w_in_sb = sb("w_in_sb", [128, 2 * HID])
        w_dw_sb = sb("w_dw_sb", [128, 2, TAPS])
        w_out_sb = sb("w_out_sb", [128, C])
        w_conv = sb("w_conv", [128, TAPS, 128], BF16)
        moments = sb("moments", [128, 2 * STEPS, 6])
        mean_var = sb("mean_var", [128, 2])
        neg_mean = sb("neg_mean", [128, 1])
        stat = sb("stat", [128, 8])
        power = sb("power", [128, 1])
        rstd = sb("rstd", [128, 1])
        w0_sb = X[1][:, 0:5, :].rearrange("p a b -> p (a b)")[:, 0:TAPS * C].rearrange("p (t c) -> p t c", t=TAPS)
        fft_sb = X[1][0:5 * PS, 8:10, :].rearrange("p a b -> p (a b)")
        pick_sb = X[1][0:5 * PS, 10, :]

        sums = [ctx.enter_context(nc.psum_tensor(f"sums{c}", [128, PS, W], F32)) for c in range(2)]
        mixed_h = [ctx.enter_context(nc.psum_tensor(f"mixed_h{i}", [128, 2, 256], F32)) for i in range(2)]
        fresh = ctx.enter_context(nc.psum_tensor("fresh", [128, 4, W], F32))
        side = ctx.enter_context(nc.psum_tensor("side", [128, 512], F32))

        weights_in = sem("weights_in")
        cleared = sem("cleared")
        signs_cleared = sem("signs_cleared")
        tables_raw = sem("tables_raw")
        tables = sem("tables")
        diagonals_done = sem("diagonals_done")
        conv_signs = sem("conv_signs")
        x_in = [sem(f"x_in{k}") for k in range(STEPS)]
        stored = [sem(f"stored{k}") for k in range(STEPS)]
        side_full = sem("side_full")
        side_free = sem("side_free")
        x1_done = sem("x1_done")
        result_done = sem("result_done")
        own_moments = sem("own_moments")
        own = sem("own")
        centred = sem("centred")
        signed = sem("signed")
        with_eps = sem("with_eps")
        rstd_done = sem("rstd_done")
        step_normed = sem("step_normed")
        mixed = sem("mixed")
        copied = sem("copied")
        framed = sem("framed")
        fresh_full = sem("fresh_full")
        kept = sem("kept")
        haloed = sem("haloed")
        started = sem("started")
        tapped = sem("tapped")
        gelu_done = sem("gelu_done")
        second_kept = sem("second_kept")
        gated = sem("gated")

        block = ctx.enter_context(nc.Block())

        def normal_parts(img, j):
            return {k: (a - img.like, part) for k, a, part in side_work(img.like, j)}

        def taps_done(img, j, c, n=None):
            ops = [2 * (TAPS - p) for p in PE_TAPS]
            n = ops[c] if n is None else n
            return img.count(sum(ops) * STRIPS, sum(ops) * j + (ops[0] if c else 0) + n)

        def step_use(img, j):
            k = j % STEPS
            return img.use(k - (STRIPS - STEP_FROM), "D1")

        @block.sync
        def _(sp):
            for dst, src in ((sq[:, :, :], square), (pick_sb, pick), (fft_sb, fft), (w_out_sb[:, :], w_out),
                             (w_dw_sb[:, :, :], w_dw.rearrange("(c p) t -> p c t", p=HID))):
                sp.dma_start(dst, src).then_inc(weights_in, 16)
            for h in range(2):
                sp.dma_start(w0_sb[64 * h:64 * h + 64], w0).then_inc(weights_in, 16)
                sp.dma_start(w_in_sb[64 * h:64 * h + 64, :], w_in).then_inc(weights_in, 16)

            def image_of(dram, img, d):
                first = 1 if img.like + d > 0 else 0
                part = dram[first:B][bass.ds(img.v + (d - first), 1)]
                return part.rearrange("a c (h r) w -> (a h) c (r w)", h=2)

            def load(img, d, k):
                sp.wait_ge(stored[k], reached(img.count(32, 0, d - 1)))
                for h in range(2):
                    src = image_of(x, img, d)
                    sp.dma_start(X[(img.like + d) % 2][64 * h:64 * h + 64, PS * k:PS * k + PS, :]
                                 .rearrange("p r w -> p (r w)"),
                                 src[h, :, k * CHUNK:(k + 1) * CHUNK]).then_inc(x_in[k], 16)

            for k in range(STEPS):
                load(Image(-1, -1), 1, k)

            def slot(img, j):
                if j >= LOAD_FROM and img.like + 2 < B:
                    if img.like == -1 and j == LOAD_FROM:
                        sp.wait_ge(tables_raw, 1)
                        sp.wait_ge(conv_signs, 2)
                        sp.wait_ge(own, 1)
                    load(img, 2, j - LOAD_FROM)
                if img.like >= 0 and j < STEPS - (STRIPS - LOAD_FROM) and img.like + 1 < B:
                    load(img, 1, j + STRIPS - LOAD_FROM)
                if img.has(j - 4):
                    s = (j - 4) % STRIPS
                    par = (img.like if j >= 4 else img.like - 1) % 2
                    h, k = s // STEPS, s % STEPS
                    sp.wait_ge(result_done, reached(img.count(2 * STRIPS, 2 * (j - 4) + 2)))
                    dst = image_of(out, img, 0 if j >= 4 else -1)
                    sp.dma_start(dst[h, :, k * CHUNK:(k + 1) * CHUNK],
                                 X[par][64 * h:64 * h + 64, PS * k:PS * k + PS, :]
                                 .rearrange("p r w -> p (r w)")).then_inc(stored[k], 16)

            over_images(sp, slot)
            for k in range(STEPS):
                sp.wait_ge(stored[k], 32 * B)

        @block.gpsimd
        def _(pool):
            nc.gpsimd.memset(signs[:], 0.0).then_inc(signs_cleared, 1)
            nc.gpsimd.memset(power[:], -0.5).then_inc(signs_cleared, 1)
            nc.gpsimd.memset(zeros[:], 0.0).then_inc(signs_cleared, 1)

            def frame(img, j, u):
                m = img.count(4 * STRIPS, 4 * j + u)
                pool.wait_ge(copied, reached(m + 1))
                if u % 2 == 0:
                    pool.wait_ge(fresh_full, reached(img.count(4 * STRIPS, 4 * (j - 2) + 2 * (u // 2) + 2)))
                if img.like == 0 and j == 0 and u == 0:
                    pool.wait_ge(tables, 1)
                for i in range(2):
                    last = nc.gpsimd.tensor_tensor(filtered[:, j % 2, 2 * u + i, :], copied_h[:, u % 2, i, :],
                                                   gains[:, :], ALU.mult)
                last.then_inc(framed, 1)

            def put(dst, row):
                return nc.gpsimd.tensor_tensor(dst, row, zeros[:, :, :].to_broadcast([128, 2, W]), ALU.subtract)

            def halo_above(img, j):
                pool.wait_ge(kept, reached(img.count(4 * STRIPS, 4 * j + 2)))
                if j % STRIPS:
                    put(plane[:, (j - 1) % RING, :, PS + 1, 1:W + 1], plane[:, j % RING, :, 1, 1:W + 1]).then_inc(haloed, 1)
                else:
                    put(plane[:, j % RING, :, 0, 1:W + 1], zeros[:, :, :].to_broadcast([128, 2, W])).then_inc(haloed, 1)

            def halo_below(img, j):
                pool.wait_ge(kept, reached(img.count(4 * STRIPS, 4 * j + 4)))
                pool.wait_ge(tapped, reached(taps_done(img, j - 3, 1)))
                if j % STRIPS < STRIPS - 1:
                    put(plane[:, (j + 1) % RING, :, 0, 1:W + 1], plane[:, j % RING, :, PS, 1:W + 1]).then_inc(haloed, 1)
                else:
                    put(plane[:, j % RING, :, PS + 1, 1:W + 1],
                        zeros[:, :, :].to_broadcast([128, 2, W])).then_inc(haloed, 1)

            def gate_part(img, j):
                pool.wait_ge(gelu_done, reached(img.strip(j + 1)))
                pool.wait_ge(second_kept, reached(img.strip(j + 1)))
                g = gate[:, j % 2, :]
                nc.gpsimd.tensor_tensor(g, second[:, :], g, ALU.mult).then_inc(gated, 1)

            def residual(img, j, q, conv):
                s = (j - 4) % STRIPS
                par = (img.like if j >= 4 else img.like - 1) % 2
                h, k = s // STEPS, s % STEPS
                pool.wait_ge(gated, reached(img.strip(j - 3)))
                if img.has(j - 1):
                    pool.wait_ge(haloed, reached(img.count(2 * STRIPS, 2 * (j - 1) + 1)))
                if img.has(j):
                    pool.wait_ge(framed, reached(img.count(4 * STRIPS, 4 * j + 2 * q + 2)))
                if conv:
                    pool.wait_ge(x1_done, reached(img.count(2 * STEPS, 2 * conv[1] + 1, conv[0])))
                pool.wait_ge(side_free, reached(img.use(j, f"P{q}")))
                px = X[par][64 * h:64 * h + 64, PS * k + 4 * q:PS * k + 4 * q + 4, :].rearrange("p y x -> p (y x)")
                nc.gpsimd.tensor_tensor(px, projected[64 * h:64 * h + 64, :], px, ALU.add).then_inc(result_done, 1)
                pool.wait_ge(result_done, reached(img.count(2 * STRIPS, 2 * (j - 4) + q + 1)))

            def conv_part(img, j, d, k, i):
                pool.wait_ge(side_free, reached(img.use(j, f"C{i}")))
                rows = X[(img.like + d) % 2][:, PS * k + 4 * i:PS * k + 4 * i + 4, :].rearrange("p r w -> p (r w)")
                nc.gpsimd.tensor_tensor(rows, from_side[:, :], rows, ALU.add).then_inc(x1_done, 1)

            def slot(img, j):
                parts = normal_parts(img, j)
                if img.has(j - 4):
                    gate_part(img, j - 4)
                if img.has(j):
                    frame(img, j, 0)
                if img.has(j - 1):
                    halo_above(img, j - 1)
                if img.has(j):
                    frame(img, j, 1)
                if "conv" in parts:
                    conv_part(img, j, *parts["conv"], 0)
                if img.has(j - 4):
                    residual(img, j, 0, parts.get("conv"))
                if img.has(j):
                    frame(img, j, 2)
                    frame(img, j, 3)
                if img.has(j - 4):
                    residual(img, j, 1, parts.get("conv"))
                if "conv" in parts:
                    conv_part(img, j, *parts["conv"], 1)
                if img.has(j - 1):
                    halo_below(img, j - 1)
                if "spread" in parts:
                    pool.wait_ge(with_eps, reached(img.count(1, 1, parts["spread"][0])))
                    nc.gpsimd.tensor_tensor(rstd[:], stat[:, 3:4], power[:], ALU.pow).then_inc(rstd_done, 1)

            pool.wait_ge(signs_cleared, 3)
            over_images(pool, slot)

        @block.scalar
        def _(act):
            act.wait_ge(weights_in, 16 * 9)
            act.wait_ge(cleared, 2)
            for h in range(2):
                nc.scalar.activation(w_conv[64 * h:64 * h + 64, :, 64 * h:64 * h + 64], w0_sb[64 * h:64 * h + 64],
                                     ACT.Sign).then_inc(conv_signs, 1)

            def keep(use, dst):
                act.wait_ge(side_full, reached(use))
                nc.scalar.copy(dst, side[:, :].rearrange("p (t f) -> p t f", t=4)).then_inc(side_free, 1)

            def keep_pixels(img, j, q, c):
                act.wait_ge(fresh_full, reached(img.count(4 * STRIPS, 4 * j + 2 * q + c + 1)))
                act.wait_ge(tapped, reached(taps_done(img, j - RING, 1)))
                nc.scalar.copy(plane[:, j % RING, c, 1 + 4 * q:5 + 4 * q, 1:W + 1], fresh[:, :, :]).then_inc(kept, 1)

            def keep_conv(img, j, d, k, i):
                act.wait_ge(side_full, reached(img.use(j, f"C{i}")))
                act.wait_ge(x1_done, reached(img.count(2 * STEPS, 2 * k + i, d)))
                nc.scalar.copy(from_side[:, :], side[:, :]).then_inc(side_free, 1)

            def keep_projection(img, j, q):
                h = ((j - 4) % STRIPS) // STEPS
                act.wait_ge(side_full, reached(img.use(j, f"P{q}")))
                act.wait_ge(result_done, reached(img.count(2 * STRIPS, 2 * (j - 4) + q)))
                nc.scalar.copy(projected[64 * h:64 * h + 64, :], side[64 * h:64 * h + 64, :]).then_inc(side_free, 1)

            def keep_second(img, j):
                act.wait_ge(tapped, reached(taps_done(img, j, 1)))
                act.wait_ge(gated, reached(img.strip(j)))
                nc.scalar.copy(second[:, :], sums[1][:, :, :].rearrange("p y x -> p (y x)")).then_inc(second_kept, 1)

            def copy_mixed(img, j, u):
                m = img.count(4 * STRIPS, 4 * j + u)
                act.wait_ge(mixed, reached(m + 1))
                act.wait_ge(framed, reached(m - 1))
                nc.scalar.copy(copied_h[:, u % 2], mixed_h[u % 2][:, :, :]).then_inc(copied, 1)

            def gelu(img, j):
                act.wait_ge(tapped, reached(taps_done(img, j, 0)))
                if img.has(j - 2):
                    act.wait_ge(side_full, reached(img.use(j + 2, "P1")))
                nc.scalar.activation(gate[:, j % 2, :], sums[0][:, :, :].rearrange("p y x -> p (y x)"),
                                     ACT.Gelu).then_inc(gelu_done, 1)

            def sign_part(img, d, k):
                Xa = X[(img.like + d) % 2]
                nc.scalar.activation(signs[:, 1 + PS * k:1 + PS * k + PS, 1:W + 1], Xa[:, PS * k:PS * k + PS, :],
                                     ACT.Sign, bias=neg_mean[:, 0:1]).then_inc(signed, 1)

            def slot(img, j):
                parts = normal_parts(img, j)
                step = parts.get("step")
                if img.has(j - 4):
                    keep_second(img, j - 4)
                if img.has(j):
                    copy_mixed(img, j, 0)
                    copy_mixed(img, j, 1)
                if img.has(j - 1):
                    keep_pixels(img, j - 1, 0, 0)
                if step:
                    keep(img.use(j, "T0"), turned[:, 0:4, :])
                if "conv" in parts:
                    keep_conv(img, j, *parts["conv"], 0)
                if img.has(j - 1):
                    keep_pixels(img, j - 1, 0, 1)
                if step:
                    keep(img.use(j, "T1"), turned[:, 4:8, :])
                if img.has(j - 3):
                    gelu(img, j - 3)
                if img.has(j - 4):
                    keep_projection(img, j, 0)
                if img.has(j):
                    copy_mixed(img, j, 2)
                    copy_mixed(img, j, 3)
                if "sign" in parts:
                    d, k = parts["sign"]
                    if k == 0:
                        Xa = X[(img.like + d) % 2]
                        act.wait_ge(centred, reached(img.count(1, 1, d)))
                        if img.like == -1:
                            act.wait_ge(signs_cleared, 3)
                        sign_part(img, d, 0)
                        nc.scalar.activation(signs[64:128, 0, 1:W + 1], Xa[0:64, H // 2 - 1, :], ACT.Sign,
                                             bias=neg_mean[0:64, 0:1]).then_inc(signed, 1)
                        nc.scalar.activation(signs[0:64, H // 2 + 1, 1:W + 1], Xa[64:128, 0, :], ACT.Sign,
                                             bias=neg_mean[64:128, 0:1]).then_inc(signed, 1)
                    if k + 1 < STEPS:
                        sign_part(img, d, k + 1)
                if step:
                    keep(img.use(j, "D0"), spectra[:, step[1], 0:4, :])
                if img.has(j - 1):
                    keep_pixels(img, j - 1, 1, 0)
                if img.has(j - 4):
                    keep_projection(img, j, 1)
                if img.has(j - 1):
                    keep_pixels(img, j - 1, 1, 1)
                if step:
                    keep(img.use(j, "D1"), spectra[:, step[1], 4:8, :])
                if "conv" in parts:
                    keep_conv(img, j, *parts["conv"], 1)

            over_images(act, slot)

        @block.tensor
        def _(pe):
            pe.wait_ge(weights_in, 16 * 9)
            nc.tensor.matmul(side[:, 0:256], pick_sb, fft_sb, start=True, stop=True).then_inc(tables_raw, 1)
            pe.wait_ge(conv_signs, 2)
            pe.wait_ge(tables, 1)

            def mix(img, j, q):
                h, k = (j % STRIPS) // STEPS, j % STEPS
                after = j >= STRIPS
                if q == 0:
                    pe.wait_ge(side_free, reached(step_use(Image(img.v + 1, img.like + 1) if after else img, j % STRIPS)))
                for u in (2 * q, 2 * q + 1):
                    pe.wait_ge(copied, reached(img.count(4 * STRIPS, 4 * j + u - 1)))
                    for i in range(2):
                        last = nc.tensor.matmul(mixed_h[u % 2][:, i, :], spectra[64 * h:64 * h + 64, k, 2 * u + i, :],
                                                w_in_sb[64 * h:64 * h + 64, :], start=True, stop=True)
                    last.then_inc(mixed, 1)

            def pixels(img, j, q, c):
                pe.wait_ge(framed, reached(img.count(4 * STRIPS, 4 * j + 2 * q + 2)))
                pe.wait_ge(kept, reached(img.count(4 * STRIPS, 4 * j + 2 * q + c)))
                for t in range(4):
                    last = nc.tensor.matmul(fresh[:, t, :], filtered[:, j % 2, 4 * q + t, HID * c:HID * c + HID],
                                            to_pixels, start=True, stop=True)
                last.then_inc(fresh_full, 1)

            def start_taps(img, j, c):
                pe.wait_ge(haloed, reached(img.count(2 * STRIPS, 2 * j + (2 if j % STRIPS == STRIPS - 1 else 3))))
                if c == 0:
                    pe.wait_ge(gelu_done, reached(img.strip(j)))
                else:
                    pe.wait_ge(second_kept, reached(img.strip(j)))
                for q in range(2):
                    for n in range(PE_TAPS[c]):
                        last = nc.tensor.matmul(sums[c][:, 4 * q:4 * q + 4, :], diagonals[:, c, n, :],
                                                plane[:, j % RING, c, 4 * q + n // 3:4 * q + n // 3 + 4, n % 3:n % 3 + W],
                                                start=(n == 0), stop=(n == PE_TAPS[c] - 1))
                last.then_inc(started, 1)

            def side_bank(use):
                pe.wait_ge(side_free, reached(use - 1))

            def project(img, j, q):
                s = (j - 4) % STRIPS
                h = s // STEPS
                side_bank(img.use(j, f"P{q}"))
                pe.wait_ge(gated, reached(img.strip(j - 3)))
                nc.tensor.matmul(side[64 * h:64 * h + 64, :], w_out_sb[:, :], gate[:, (j - 4) % 2, 512 * q:512 * q + 512],
                                 start=True, stop=True).then_inc(side_full, 1)

            def turn(img, j, d, k, i):
                side_bank(img.use(j, f"T{i}"))
                if i == 0:
                    pe.wait_ge(step_normed, reached(img.count(STEPS, k + 1, d)))
                for t in range(4):
                    last = nc.tensor.transpose(side[:, 128 * t:128 * t + 128], normed[:, 4 * i + t, :], ident)
                last.then_inc(side_full, 1)

            def spectrum(img, j, i):
                side_bank(img.use(j, f"D{i}"))
                pe.wait_ge(side_free, reached(img.use(j, f"T{i}")))
                for t in range(4):
                    last = nc.tensor.matmul(side[:, 128 * t:128 * t + 128], turned[:, 4 * i + t, :], to_spectrum,
                                            start=True, stop=True)
                last.then_inc(side_full, 1)

            def conv(img, j, d, k, i):
                side_bank(img.use(j, f"C{i}"))
                pe.wait_ge(signed, reached(img.count(STEPS + 2, min(k + 1, STEPS - 1) + 3, d)))
                row = PS * k + 4 * i
                for tap in range(TAPS):
                    dy, dx = tap // 3, tap % 3
                    last = nc.tensor.matmul(side[:, :], w_conv[:, tap, :], signs[:, row + dy:row + dy + 4, dx:dx + W],
                                            start=(tap == 0), stop=(tap == TAPS - 1))
                last.then_inc(side_full, 1)

            def group_mean(img, j, name, col, which, d):
                side_bank(img.use(j, name))
                pe.wait_ge(own_moments, reached(img.count(3, which, d)))
                nc.tensor.matmul(side[:, 0:1], average, col, start=True, stop=True).then_inc(side_full, 1)

            def slot(img, j):
                parts = normal_parts(img, j)
                if img.has(j - 1):
                    pixels(img, j - 1, 0, 0)
                if "step" in parts:
                    turn(img, j, *parts["step"], 0)
                if "conv" in parts:
                    conv(img, j, *parts["conv"], 0)
                if img.has(j - 1):
                    pixels(img, j - 1, 0, 1)
                if "step" in parts:
                    turn(img, j, *parts["step"], 1)
                if img.has(j - 3):
                    start_taps(img, j - 3, 1)
                if img.has(j - 4):
                    project(img, j, 0)
                if img.has(j):
                    mix(img, j, 1)
                if "mean" in parts:
                    group_mean(img, j, "M", mean_var[:, 0:1], 1, parts["mean"][0])
                if "spread" in parts:
                    group_mean(img, j, "S0", mean_var[:, 0:1], 2, parts["spread"][0])
                if img.has(j - 2):
                    start_taps(img, j - 2, 0)
                if "spread" in parts:
                    group_mean(img, j, "S1", stat[:, 2:3], 3, parts["spread"][0])
                if "step" in parts:
                    spectrum(img, j, 0)
                if img.has(j - 1):
                    pixels(img, j - 1, 1, 0)
                if img.has(j - 4):
                    project(img, j, 1)
                if img.has(j - 1):
                    pixels(img, j - 1, 1, 1)
                if "step" in parts:
                    spectrum(img, j, 1)
                if "conv" in parts:
                    conv(img, j, *parts["conv"], 1)
                if img.has(j + 1) and img.like >= 0:
                    mix(img, j + 1, 0)

            def before():
                pe.wait_ge(diagonals_done, sum(PE_TAPS))
                mix(Image(0, 0), 0, 0)

            over_images(pe, slot, before)

        @block.vector
        def _(dve):
            nc.vector.memset(w_conv[:], 0.0).then_inc(cleared, 1)
            nc.vector.memset(plane[:], 0.0).then_inc(cleared, 1)
            dve.wait_ge(weights_in, 16 * 9)
            for c in range(2):
                for n in range(PE_TAPS[c]):
                    nc.vector.tensor_scalar(diagonals[:, c, n, :], ident, w_dw_sb[:, c, n:n + 1], None,
                                            ALU.mult).then_inc(diagonals_done, 1)
            dve.wait_ge(tables_raw, 1)
            nc.vector.tensor_copy(gains[:, :], side[:, 0:256]).then_inc(tables, 1)

            def chunk_moments(Xa, k, i):
                return nc.vector.bn_stats(moments[:, 2 * k + i, :],
                                          Xa[:, PS * k + 4 * i:PS * k + 4 * i + 4, :].rearrange("p r w -> p (r w)"))

            def stat_part(img, d, k):
                dve.wait_ge(x_in[k], reached(img.count(32, 32, d)))
                if k == 0:
                    dve.wait_ge(own_moments, reached(img.count(3, 2, d - 1)))
                for i in range(2):
                    last = chunk_moments(X[(img.like + d) % 2], k, i)
                if k == STEPS - 1:
                    last.then_inc(own, 1)

            def aggregate_after_wait():
                nc.vector.memset(stat[:, 6:7], 0.0)

            def aggregate(img, j, d, which):
                dve.wait_ge(own, reached(img.count(3, which, d)))
                nc.vector.memset(stat[:, 6:7], 0.0)
                nc.vector.bn_aggr(mean_var[:, :], moments[:, :, :].rearrange("p n s -> p (n s)")).then_inc(own_moments, 1)

            def mean_part(img, j, d):
                dve.wait_ge(side_full, reached(img.use(j, "M")))
                nc.vector.tensor_scalar(neg_mean[:, :], side[:, 0:1], -1.0, None, ALU.mult).then_inc(centred, 1)
                dve.wait_ge(centred, reached(img.count(1, 1, d)))
                nc.vector.tensor_copy(stat[:, 4:5], side[:, 0:1]).then_inc(side_free, 1)

            def spread_part(img, j, d):
                dve.wait_ge(side_full, reached(img.use(j, "S0")))
                dve.wait_ge(own_moments, reached(img.count(3, 2, d)))
                nc.vector.tensor_copy(stat[:, 0:1], side[:, 0:1]).then_inc(own, 1)
                nc.vector.tensor_tensor(stat[:, 1:2], side[:, 0:1], mean_var[:, 0:1], ALU.subtract).then_inc(side_free, 1)
                dve.wait_ge(side_free, reached(img.use(j, "S0")))
                nc.vector.scalar_tensor_tensor(out=stat[:, 2:3], in0=stat[:, 1:2], scalar=stat[:, 1:2],
                                               in1=mean_var[:, 1:2], op0=ALU.mult, op1=ALU.add).then_inc(own_moments, 1)

            def variance_part(img, j, d):
                dve.wait_ge(side_full, reached(img.use(j, "S1")))
                nc.vector.tensor_scalar(stat[:, 3:4], side[:, 0:1], EPS, None, ALU.add).then_inc(with_eps, 1)
                dve.wait_ge(with_eps, reached(img.count(1, 1, d)))
                nc.vector.tensor_copy(stat[:, 5:6], side[:, 0:1]).then_inc(side_free, 1)

            def normalise(img, j, d, k):
                dve.wait_ge(rstd_done, reached(img.count(1, 1, d)))
                dve.wait_ge(own, reached(img.count(3, 3, d)))
                if k > 0:
                    dve.wait_ge(side_full, reached(img.use(j - 1, "T1")))
                elif img.like + d > 0:
                    dve.wait_ge(side_full, reached(img.use(j - (STRIPS - STEPS) - 1, "T1")))
                nc.vector.tensor_scalar(normed[:, :, :], X[(img.like + d) % 2][:, PS * k:PS * k + PS, :],
                                        stat[:, 0:1], rstd[:, 0:1], ALU.subtract, ALU.mult).then_inc(step_normed, 1)

            def conv_moments(img, d, k, i):
                dve.wait_ge(x1_done, reached(img.count(2 * STEPS, 2 * k + i + 1, d)))
                last = chunk_moments(X[(img.like + d) % 2], k, i)
                if (k, i) == (STEPS - 1, 1):
                    last.then_inc(own, 1)

            def add_taps(img, j, c, first, last):
                if first == 0:
                    dve.wait_ge(started, reached(img.count(2 * STRIPS, 2 * j + c + 1)))
                for n in range(first, last):
                    tap, q = PE_TAPS[c] + n // 2, n % 2
                    if n >= 2:
                        dve.wait_ge(tapped, reached(taps_done(img, j, c, n - 1)))
                    rows = sums[c][:, 4 * q:4 * q + 4, :]
                    nc.vector.scalar_tensor_tensor(
                        out=rows,
                        in0=plane[:, j % RING, c, 4 * q + tap // 3:4 * q + tap // 3 + 4, tap % 3:tap % 3 + W],
                        scalar=w_dw_sb[:, c, tap:tap + 1], in1=rows, op0=ALU.mult, op1=ALU.add).then_inc(tapped, 1)

            def slot(img, j):
                parts = normal_parts(img, j)

                def taps(c, half):
                    n = TAPS - PE_TAPS[c]
                    if img.has(j - 3):
                        add_taps(img, j - 3, c, n * half, n * (half + 1))

                if "step" in parts:
                    normalise(img, j, *parts["step"])
                taps(0, 0)
                if "late" in parts:
                    conv_moments(img, *parts["late"], 1)
                if "spread" in parts:
                    aggregate(img, j, parts["spread"][0], 2)
                if "stat" in parts:
                    stat_part(img, *parts["stat"])
                if "mean" in parts:
                    aggregate(img, j, parts["mean"][0], 1)
                taps(0, 1)
                if "mean" in parts:
                    mean_part(img, j, parts["mean"][0])
                if "spread" in parts:
                    spread_part(img, j, parts["spread"][0])
                taps(1, 0)
                if "conv" in parts:
                    conv_moments(img, *parts["conv"], 0)
                if "spread" in parts:
                    variance_part(img, j, parts["spread"][0])
                taps(1, 1)

            for k in range(STRIPS - STAT_FROM):
                stat_part(Image(-1, -1), 1, k)
            over_images(dve, slot)


def fourier_constants():
    import numpy as np
    y, x = np.meshgrid(np.arange(PS), np.arange(PS), indexing="ij")
    basis, pick = [], []
    for v in range(PS // 2 + 1):
        for u in range(PS):
            paired = v in (0, PS // 2)
            if paired and u > PS // 2:
                continue
            angle = 2 * np.pi * (u * y + v * x) / PS
            own = np.zeros((PS, PS // 2 + 1))
            if paired:
                own[u, v] += 0.5
                own[-u % PS, v] += 0.5
            else:
                own[u, v] = 1
            if paired and u in (0, PS // 2):
                members = [np.cos(angle) / PS]
            else:
                members = [f(angle) * np.sqrt(2) / PS for f in (np.cos, np.sin)]
            for q in members:
                basis.append(q.ravel())
                pick.append(own.ravel())
    basis, pick = np.stack(basis), np.stack(pick, 1)
    ident = np.eye(128)
    average = np.zeros((128, 128))
    for p in range(128):
        for o in range(128):
            if (p % C) // 2 == (o % C) // 2:
                average[p, o] = 0.25
    to_pixels = np.kron(np.eye(2), basis)
    square = np.stack([ident, average, to_pixels.T, to_pixels], 1)
    return {"square": square.astype(np.float32), "pick": np.concatenate([pick, pick], 1).astype(np.float32)}


def kernel(**inputs):
    import numpy as np
    import concourse.bacc as bacc
    from concourse.bass_utils import run_bass_kernel_spmd as run

    a = {k: np.asarray(v) for k, v in inputs.items()}
    arrays = {
        "x": a["x"],
        "w0": a["L0_conv_weight"].transpose(1, 2, 3, 0).reshape(C, TAPS, C),
        "w_in": a["L1_conv_w_in"].T,
        "w_dw": a["L1_conv_w_dw"].reshape(2 * HID, TAPS),
        "fft": a["L1_conv_fft_params"].reshape(2 * HID, 5 * PS).T,
        "w_out": a["L1_conv_w_out"].T,
    }
    arrays.update(fourier_constants())
    arrays = {k: np.ascontiguousarray(v) for k, v in arrays.items()}
    nc = bacc.Bacc("TRN2", target_bir_lowering=False, num_devices=1)
    args = [nc.dram_tensor(f"in_{k}", v.shape, mybir.dt.from_np(v.dtype), kind="ExternalInput").ap()
            for k, v in arrays.items()]
    out = nc.dram_tensor("result", a["x"].shape, F32, kind="ExternalOutput").ap()
    preact_layers(nc, *args, out)
    got = run(nc, [{f"in_{k}": v for k, v in arrays.items()}], core_ids=[0])
    return got.results[0]["result"]
```

```python
from contextlib import ExitStack

import concourse.bass as bass
from concourse import mybir

F32 = mybir.dt.float32
BF16 = mybir.dt.bfloat16
ALU = mybir.AluOpType
ACT = mybir.ActivationFunctionType

B, C, H, W = 32, 64, 128, 128
HID = 128
PS = 8
STRIPS = H // PS
STEPS = STRIPS // 2
CHUNK = PS * W
TILES = PS
TAPS = 9
PE_TAPS = (2, 2)
OTHER_TAPS = (0, 1)
RING = 4
EPS = 1e-5

STAT_FROM, CONV_FROM, STEP_FROM, LOAD_FROM = 14, 6, 15, 13
MEAN_SLOT, SPREAD_SLOT = 5, 14


def side_work(b, j):
    out = []
    if j >= STEP_FROM:
        out.append(("step", b + 1, j - STEP_FROM))
    if j < STEP_FROM - STEPS:
        out.append(("step", b, j + STRIPS - STEP_FROM))
    if j >= STAT_FROM:
        out.append(("stat", b + 2, j - STAT_FROM))
    if j < STAT_FROM - STEPS:
        out.append(("stat", b + 1, j + STRIPS - STAT_FROM))
    if CONV_FROM <= j < CONV_FROM + STEPS:
        out.append(("conv", b + 1, j - CONV_FROM))
    if CONV_FROM <= j - 1 < CONV_FROM + STEPS:
        out.append(("late", b + 1, j - 1 - CONV_FROM))
    if CONV_FROM <= j + 1 < CONV_FROM + STEPS:
        out.append(("sign", b + 1, j + 1 - CONV_FROM))
    if j == MEAN_SLOT:
        out.append(("mean", b + 1, 0))
    if j == SPREAD_SLOT:
        out.append(("spread", b + 1, 0))
    return [w for w in out if 0 <= w[1] < B]


def bank_uses():
    number, n = {}, 0
    for b in range(-1, B + 1):
        for j in range(STRIPS):
            kinds = [k for k, _, _ in side_work(b, j)]
            project = 4 <= b * STRIPS + j < B * STRIPS + 4
            for name, there in (("T0", "step" in kinds), ("C0", "conv" in kinds),
                                ("D0", "step" in kinds), ("M", "mean" in kinds),
                                ("S0", "spread" in kinds), ("P", project),
                                ("S1", "spread" in kinds), ("T1", "step" in kinds),
                                ("C1", "conv" in kinds), ("D1", "step" in kinds)):
                if there:
                    n += 1
                    number[b, j, name] = n
    return number


USES = bank_uses()
USES_PER_IMAGE = USES[2, 0, "P"] - USES[1, 0, "P"]


class Image:

    def __init__(self, v, like):
        self.v, self.like = v, like

    def count(self, per_image, more, d=0):
        return self.v * per_image + (per_image * d + more)

    def use(self, j, name):
        b, j = (self.like, j) if j >= 0 else (self.like - 1, j + STRIPS)
        return (self.v - self.like) * USES_PER_IMAGE + USES[b, j, name]

    def strip(self, j):
        return self.v * STRIPS + j

    def has(self, j):
        return 0 <= self.like * STRIPS + j < B * STRIPS


def vector_taps(c):
    return TAPS - PE_TAPS[c] - OTHER_TAPS[c]


def reached(value):
    return max(value, 0) if isinstance(value, int) else value


def over_images(eng, slot, before=None):
    for j in range(STRIPS):
        slot(Image(-1, -1), j)
    if before:
        before()
    for j in range(STRIPS):
        slot(Image(0, 0), j)
    with eng.Fori(0, (B - 4) // 2) as i:
        for parity in (1, 2):
            for j in range(STRIPS):
                slot(Image(i * 2 + parity, parity), j)
    for b in range(B - 3, B):
        for j in range(STRIPS):
            slot(Image(b, b), j)
    for j in range(4):
        slot(Image(B, B), j)


def preact_layers(nc, x, w0, w_in, w_dw, fft, w_out, square, pick, out):
    ctx = ExitStack()
    with ctx:
        def sb(name, shape, dt=F32):
            return ctx.enter_context(nc.sbuf_tensor(name, shape, dt))

        def sem(name):
            return ctx.enter_context(nc.semaphore(name))

        X = [sb(f"X{i}", [128, H // 2, W]) for i in range(2)]
        spectra = sb("spectra", [128, STEPS, TILES, 128])
        signs = sb("signs", [128, H // 2 + 2, W + 2], BF16)
        copied_h = sb("copied_h", [128, 2, 2, 2 * HID])
        filtered = sb("filtered", [128, 2, TILES, 2 * HID])
        plane = sb("plane", [128, RING, 2, PS + 2, W + 2])
        gate = sb("gate", [128, 2, CHUNK])
        second = sb("second", [128, PS, W])
        product = sb("product", [128, PS, W])
        from_side = sb("from_side", [128, 512])
        projected = sb("projected", [128, 2, 512])
        turned = sb("turned", [128, 4, 128])
        zeros = sb("zeros", [128, 1, 1])
        sq = sb("sq", [128, 4, 128])
        ident, average, to_spectrum, to_pixels = (sq[:, i, :] for i in range(4))
        gains = sb("gains", [128, 2 * HID])
        diagonals = sb("diagonals", [128, 2, max(PE_TAPS), 128])
        w_in_sb = sb("w_in_sb", [128, 2 * HID])
        w_dw_sb = sb("w_dw_sb", [128, 2, TAPS])
        w_out_sb = sb("w_out_sb", [128, C])
        w_conv = sb("w_conv", [128, TAPS, 128], BF16)
        moments = sb("moments", [128, 2 * STEPS, 6])
        mean_var = sb("mean_var", [128, 2])
        x_sums = sb("x_sums", [128, STEPS])
        shift = sb("shift", [128, 1])
        neg_mean = sb("neg_mean", [128, 1])
        stat = sb("stat", [128, 8])
        power = sb("power", [128, 1])
        rstd = sb("rstd", [128, 1])
        w0_sb = X[1][:, 0:5, :].rearrange("p a b -> p (a b)")[:, 0:TAPS * C].rearrange("p (t c) -> p t c", t=TAPS)
        fft_sb = X[1][0:5 * PS, 8:10, :].rearrange("p a b -> p (a b)")
        pick_sb = X[1][0:5 * PS, 10, :]

        sums = [ctx.enter_context(nc.psum_tensor(f"sums{c}", [128, PS, W], F32)) for c in range(2)]
        mixed_h = [ctx.enter_context(nc.psum_tensor(f"mixed_h{i}", [128, 2, 256], F32)) for i in range(2)]
        fresh = ctx.enter_context(nc.psum_tensor("fresh", [128, 4, W], F32))
        side = ctx.enter_context(nc.psum_tensor("side", [128, 512], F32))

        weights_in = sem("weights_in")
        cleared = sem("cleared")
        signs_cleared = sem("signs_cleared")
        tables_raw = sem("tables_raw")
        tables = sem("tables")
        diagonals_done = sem("diagonals_done")
        conv_signs = sem("conv_signs")
        x_in = [sem(f"x_in{k}") for k in range(STEPS)]
        stored = [sem(f"stored{k}") for k in range(STEPS)]
        side_full = sem("side_full")
        side_free = sem("side_free")
        x1_done = sem("x1_done")
        result_done = sem("result_done")
        own_moments = sem("own_moments")
        own = sem("own")
        summed = sem("summed")
        centred = sem("centred")
        signed = sem("signed")
        with_eps = sem("with_eps")
        rstd_done = sem("rstd_done")
        mixed = sem("mixed")
        copied = sem("copied")
        framed = sem("framed")
        fresh_full = sem("fresh_full")
        kept = sem("kept")
        haloed = sem("haloed")
        started = sem("started")
        tapped = sem("tapped")
        gelu_done = sem("gelu_done")
        second_kept = sem("second_kept")
        product_done = sem("product_done")
        joined = sem("joined")
        gated = sem("gated")

        block = ctx.enter_context(nc.Block())

        def normal_parts(img, j):
            return {k: (a - img.like, part) for k, a, part in side_work(img.like, j)}

        def taps_done(img, j, c, n=None):
            ops = [2 * vector_taps(half) for half in range(2)]
            n = ops[c] if n is None else n
            return img.count(sum(ops) * STRIPS, sum(ops) * j + (ops[0] if c else 0) + n)

        def step_use(img, j):
            k = j % STEPS
            return img.use(k - (STRIPS - STEP_FROM), "D1")

        @block.sync
        def _(sp):
            for dst, src in ((sq[:, :, :], square), (pick_sb, pick), (fft_sb, fft), (w_out_sb[:, :], w_out),
                             (w_dw_sb[:, :, :], w_dw.rearrange("(c p) t -> p c t", p=HID))):
                sp.dma_start(dst, src).then_inc(weights_in, 16)
            for h in range(2):
                sp.dma_start(w0_sb[64 * h:64 * h + 64], w0).then_inc(weights_in, 16)
                sp.dma_start(w_in_sb[64 * h:64 * h + 64, :], w_in).then_inc(weights_in, 16)

            def image_of(dram, img, d):
                first = 1 if img.like + d > 0 else 0
                part = dram[first:B][bass.ds(img.v + (d - first), 1)]
                return part.rearrange("a c (h r) w -> (a h) c (r w)", h=2)

            def load(img, d, k):
                sp.wait_ge(stored[k], reached(img.count(32, 0, d - 1)))
                for h in range(2):
                    src = image_of(x, img, d)
                    sp.dma_start(X[(img.like + d) % 2][64 * h:64 * h + 64, PS * k:PS * k + PS, :]
                                 .rearrange("p r w -> p (r w)"),
                                 src[h, :, k * CHUNK:(k + 1) * CHUNK]).then_inc(x_in[k], 16)

            for k in range(STEPS):
                load(Image(-1, -1), 1, k)

            def slot(img, j):
                if j >= LOAD_FROM and img.like + 2 < B:
                    if img.like == -1 and j == LOAD_FROM:
                        sp.wait_ge(tables_raw, 1)
                        sp.wait_ge(conv_signs, 2)
                        sp.wait_ge(summed, STEPS)
                    load(img, 2, j - LOAD_FROM)
                if img.like >= 0 and j < STEPS - (STRIPS - LOAD_FROM) and img.like + 1 < B:
                    load(img, 1, j + STRIPS - LOAD_FROM)
                if img.has(j - 4):
                    s = (j - 4) % STRIPS
                    par = (img.like if j >= 4 else img.like - 1) % 2
                    h, k = s // STEPS, s % STEPS
                    sp.wait_ge(result_done, reached(img.strip(j - 3)))
                    dst = image_of(out, img, 0 if j >= 4 else -1)
                    sp.dma_start(dst[h, :, k * CHUNK:(k + 1) * CHUNK],
                                 X[par][64 * h:64 * h + 64, PS * k:PS * k + PS, :]
                                 .rearrange("p r w -> p (r w)")).then_inc(stored[k], 16)

            over_images(sp, slot)
            for k in range(STEPS):
                sp.wait_ge(stored[k], 32 * B)

        @block.gpsimd
        def _(pool):
            nc.gpsimd.memset(signs[:], 0.0).then_inc(signs_cleared, 1)
            nc.gpsimd.memset(power[:], -0.5).then_inc(signs_cleared, 1)
            nc.gpsimd.memset(zeros[:], 0.0).then_inc(signs_cleared, 1)

            def frame(img, j, u):
                m = img.count(4 * STRIPS, 4 * j + u)
                pool.wait_ge(copied, reached(m + 1))
                if u % 2 == 0:
                    pool.wait_ge(fresh_full, reached(img.count(4 * STRIPS, 4 * (j - 2) + 2 * (u // 2) + 2)))
                if img.like == 0 and j == 0 and u == 0:
                    pool.wait_ge(tables, 1)
                for i in range(2):
                    last = nc.gpsimd.tensor_tensor(filtered[:, j % 2, 2 * u + i, :], copied_h[:, u % 2, i, :],
                                                   gains[:, :], ALU.mult)
                last.then_inc(framed, 1)

            def put(dst, row):
                return nc.gpsimd.tensor_tensor(dst, row, zeros[:, :, :].to_broadcast([128, 2, W]), ALU.subtract)

            def halo_above(img, j):
                pool.wait_ge(kept, reached(img.count(4 * STRIPS, 4 * j + 2)))
                if j % STRIPS:
                    put(plane[:, (j - 1) % RING, :, PS + 1, 1:W + 1], plane[:, j % RING, :, 1, 1:W + 1]).then_inc(haloed, 1)
                else:
                    put(plane[:, j % RING, :, 0, 1:W + 1], zeros[:, :, :].to_broadcast([128, 2, W])).then_inc(haloed, 1)

            def halo_below(img, j):
                pool.wait_ge(kept, reached(img.count(4 * STRIPS, 4 * j + 4)))
                pool.wait_ge(tapped, reached(taps_done(img, j - 3, 1)))
                if j % STRIPS < STRIPS - 1:
                    put(plane[:, (j + 1) % RING, :, 0, 1:W + 1], plane[:, j % RING, :, PS, 1:W + 1]).then_inc(haloed, 1)
                else:
                    put(plane[:, j % RING, :, PS + 1, 1:W + 1],
                        zeros[:, :, :].to_broadcast([128, 2, W])).then_inc(haloed, 1)

            def last_tap(img, j):
                pool.wait_ge(second_kept, reached(img.strip(j + 1)))
                pool.wait_ge(product_done, reached(img.strip(j + 1)))
                nc.gpsimd.tensor_tensor(second[:, :, :], product[:, :, :], second[:, :, :], ALU.add).then_inc(joined, 1)

            def gate_part(img, j):
                pool.wait_ge(gelu_done, reached(img.strip(j + 1)))
                pool.wait_ge(joined, reached(img.strip(j + 1)))
                g = gate[:, j % 2, :]
                nc.gpsimd.tensor_tensor(g, second[:, :, :].rearrange("p y x -> p (y x)"), g, ALU.mult).then_inc(gated, 1)

            def residual(img, j):
                s = (j - 4) % STRIPS
                par = (img.like if j >= 4 else img.like - 1) % 2
                h, k = s // STEPS, s % STEPS
                pool.wait_ge(gated, reached(img.strip(j - 3)))
                if img.has(j - 1):
                    pool.wait_ge(haloed, reached(img.count(2 * STRIPS, 2 * (j - 1) + 1)))
                if img.has(j):
                    pool.wait_ge(framed, reached(img.count(4 * STRIPS, 4 * j + 2)))
                pool.wait_ge(side_free, reached(img.use(j, "P")))
                px = X[par][64 * h:64 * h + 64, PS * k:PS * k + PS, :].rearrange("p y x -> p (y x)")
                nc.gpsimd.tensor_tensor(px, projected[64 * h:64 * h + 64, :, :].rearrange("p q n -> p (q n)"), px,
                                        ALU.add).then_inc(result_done, 1)
                pool.wait_ge(result_done, reached(img.strip(j - 3)))

            def conv_part(img, j, d, k, i):
                pool.wait_ge(side_free, reached(img.use(j, f"C{i}")))
                rows = X[(img.like + d) % 2][:, PS * k + 4 * i:PS * k + 4 * i + 4, :].rearrange("p r w -> p (r w)")
                nc.gpsimd.tensor_tensor(rows, from_side[:, :], rows, ALU.add).then_inc(x1_done, 1)

            def slot(img, j):
                parts = normal_parts(img, j)
                if img.has(j - 4):
                    last_tap(img, j - 4)
                    gate_part(img, j - 4)
                if img.has(j):
                    frame(img, j, 0)
                if img.has(j - 1):
                    halo_above(img, j - 1)
                if "conv" in parts:
                    conv_part(img, j, *parts["conv"], 0)
                if img.has(j):
                    frame(img, j, 1)
                if img.has(j - 4):
                    residual(img, j)
                if img.has(j):
                    frame(img, j, 2)
                    frame(img, j, 3)
                if "conv" in parts:
                    conv_part(img, j, *parts["conv"], 1)
                if img.has(j - 1):
                    halo_below(img, j - 1)
                if "spread" in parts:
                    pool.wait_ge(with_eps, reached(img.count(1, 1, parts["spread"][0])))
                    d = parts["spread"][0]
                    nc.gpsimd.tensor_tensor(rstd[:], stat[:, 3:4], power[:], ALU.pow).then_inc(rstd_done, 1)
                    pool.wait_ge(rstd_done, reached(img.count(2, 1, d)))
                    pool.wait_ge(own, reached(img.count(2, 2, d)))
                    nc.gpsimd.tensor_tensor(shift[:], stat[:, 0:1], rstd[:], ALU.mult).then_inc(rstd_done, 1)

            pool.wait_ge(signs_cleared, 3)
            pool.wait_ge(weights_in, 16 * 9)
            over_images(pool, slot)

        @block.scalar
        def _(act):
            act.wait_ge(weights_in, 16 * 9)
            act.wait_ge(cleared, 2)
            for h in range(2):
                nc.scalar.activation(w_conv[64 * h:64 * h + 64, :, 64 * h:64 * h + 64], w0_sb[64 * h:64 * h + 64],
                                     ACT.Sign).then_inc(conv_signs, 1)

            def keep(use, dst):
                act.wait_ge(side_full, reached(use))
                nc.scalar.copy(dst, side[:, :].rearrange("p (t f) -> p t f", t=4)).then_inc(side_free, 1)

            def keep_pixels(img, j, q, c):
                act.wait_ge(fresh_full, reached(img.count(4 * STRIPS, 4 * j + 2 * q + c + 1)))
                act.wait_ge(tapped, reached(taps_done(img, j - RING, 1)))
                nc.scalar.copy(plane[:, j % RING, c, 1 + 4 * q:5 + 4 * q, 1:W + 1], fresh[:, :, :]).then_inc(kept, 1)

            def keep_conv(img, j, d, k, i):
                act.wait_ge(side_full, reached(img.use(j, f"C{i}")))
                act.wait_ge(x1_done, reached(img.count(2 * STEPS, 2 * k + i, d)))
                nc.scalar.copy(from_side[:, :], side[:, :]).then_inc(side_free, 1)

            def keep_projection(img, j):
                h = ((j - 4) % STRIPS) // STEPS
                act.wait_ge(side_full, reached(img.use(j, "P")))
                act.wait_ge(result_done, reached(img.strip(j - 4)))
                nc.scalar.copy(projected[64 * h:64 * h + 64, 0, :], side[64 * h:64 * h + 64, :])
                nc.scalar.copy(projected[64 * h:64 * h + 64, 1, :], side[64 - 64 * h:128 - 64 * h, :]).then_inc(side_free, 1)

            def keep_spectrum(img, j, d, k, i):
                act.wait_ge(side_full, reached(img.use(j, f"D{i}")))
                act.wait_ge(rstd_done, reached(img.count(2, 2, d)))
                bank = side[:, :].rearrange("p (t f) -> p t f", f=PS * PS)
                dst = spectra[:, k, 4 * i:4 * i + 4, :].rearrange("p t (m f) -> p (t m) f", m=2)
                nc.scalar.activation(dst[:, :, 0:1], bank[:, :, 0:1], ACT.Identity, bias=shift[:, 0:1], scale=rstd[:, 0:1])
                nc.scalar.activation(dst[:, :, 1:PS * PS], bank[:, :, 1:PS * PS], ACT.Identity,
                                     scale=rstd[:, 0:1]).then_inc(side_free, 1)

            def stat_part(img, d, k):
                act.wait_ge(x_in[k], reached(img.count(32, 32, d)))
                if k == 0:
                    act.wait_ge(centred, reached(img.count(1, 0, d)))
                rows = X[(img.like + d) % 2][:, PS * k:PS * k + PS, :].rearrange("p r w -> p (r w)")
                nc.scalar.activation(rows, rows, ACT.Copy, accum_out=x_sums[:, k:k + 1]).then_inc(summed, 1)

            def keep_second(img, j):
                act.wait_ge(tapped, reached(taps_done(img, j, 1)))
                act.wait_ge(gated, reached(img.strip(j)))
                nc.scalar.copy(second[:, :, :], sums[1][:, :, :]).then_inc(second_kept, 1)

            def multiply_last_tap(img, j):
                act.wait_ge(started, reached(img.count(2 * STRIPS, 2 * j + 2)))
                act.wait_ge(joined, reached(img.strip(j)))
                tap = TAPS - 1
                nc.scalar.activation(product[:, :, :],
                                     plane[:, j % RING, 1, tap // 3:tap // 3 + PS, tap % 3:tap % 3 + W], ACT.Copy,
                                     scale=w_dw_sb[:, 1, tap:tap + 1]).then_inc(product_done, 1)

            def copy_mixed(img, j, u):
                m = img.count(4 * STRIPS, 4 * j + u)
                act.wait_ge(mixed, reached(m + 1))
                act.wait_ge(framed, reached(m - 1))
                nc.scalar.copy(copied_h[:, u % 2], mixed_h[u % 2][:, :, :]).then_inc(copied, 1)

            def gelu(img, j):
                act.wait_ge(tapped, reached(taps_done(img, j, 0)))
                if img.has(j - 2):
                    act.wait_ge(side_full, reached(img.use(j + 2, "P")))
                nc.scalar.activation(gate[:, j % 2, :], sums[0][:, :, :].rearrange("p y x -> p (y x)"),
                                     ACT.Gelu).then_inc(gelu_done, 1)

            def sign_part(img, d, k):
                Xa = X[(img.like + d) % 2]
                nc.scalar.activation(signs[:, 1 + PS * k:1 + PS * k + PS, 1:W + 1], Xa[:, PS * k:PS * k + PS, :],
                                     ACT.Sign, bias=neg_mean[:, 0:1]).then_inc(signed, 1)

            def slot(img, j):
                parts = normal_parts(img, j)
                step = parts.get("step")
                if img.has(j - 4):
                    keep_second(img, j - 4)
                if img.has(j):
                    copy_mixed(img, j, 0)
                    copy_mixed(img, j, 1)
                if img.has(j - 1):
                    keep_pixels(img, j - 1, 0, 0)
                if step:
                    keep(img.use(j, "T0"), turned[:, :, :])
                if "stat" in parts:
                    stat_part(img, *parts["stat"])
                if "conv" in parts:
                    keep_conv(img, j, *parts["conv"], 0)
                if img.has(j - 1):
                    keep_pixels(img, j - 1, 0, 1)
                if step:
                    keep_spectrum(img, j, *step, 0)
                if img.has(j - 4):
                    keep_projection(img, j)
                if img.has(j - 3):
                    gelu(img, j - 3)
                if img.has(j):
                    copy_mixed(img, j, 2)
                    copy_mixed(img, j, 3)
                if "sign" in parts:
                    d, k = parts["sign"]
                    if k == 0:
                        Xa = X[(img.like + d) % 2]
                        act.wait_ge(centred, reached(img.count(1, 1, d)))
                        if img.like == -1:
                            act.wait_ge(signs_cleared, 3)
                        sign_part(img, d, 0)
                        nc.scalar.activation(signs[64:128, 0, 1:W + 1], Xa[0:64, H // 2 - 1, :], ACT.Sign,
                                             bias=neg_mean[0:64, 0:1]).then_inc(signed, 1)
                        nc.scalar.activation(signs[0:64, H // 2 + 1, 1:W + 1], Xa[64:128, 0, :], ACT.Sign,
                                             bias=neg_mean[64:128, 0:1]).then_inc(signed, 1)
                    if k + 1 < STEPS:
                        sign_part(img, d, k + 1)
                if step:
                    keep(img.use(j, "T1"), turned[:, :, :])
                if img.has(j - 1):
                    keep_pixels(img, j - 1, 1, 0)
                if "conv" in parts:
                    keep_conv(img, j, *parts["conv"], 1)
                if img.has(j - 3):
                    multiply_last_tap(img, j - 3)
                if step:
                    keep_spectrum(img, j, *step, 1)
                if img.has(j - 1):
                    keep_pixels(img, j - 1, 1, 1)

            for k in range(STRIPS - STAT_FROM):
                stat_part(Image(-1, -1), 1, k)
            over_images(act, slot)

        @block.tensor
        def _(pe):
            pe.wait_ge(weights_in, 16 * 9)
            nc.tensor.matmul(side[:, 0:256], pick_sb, fft_sb, start=True, stop=True).then_inc(tables_raw, 1)
            pe.wait_ge(conv_signs, 2)
            pe.wait_ge(tables, 1)

            def mix(img, j, q):
                h, k = (j % STRIPS) // STEPS, j % STEPS
                after = j >= STRIPS
                if q == 0:
                    pe.wait_ge(side_free, reached(step_use(Image(img.v + 1, img.like + 1) if after else img, j % STRIPS)))
                for u in (2 * q, 2 * q + 1):
                    pe.wait_ge(copied, reached(img.count(4 * STRIPS, 4 * j + u - 1)))
                    for i in range(2):
                        last = nc.tensor.matmul(mixed_h[u % 2][:, i, :], spectra[64 * h:64 * h + 64, k, 2 * u + i, :],
                                                w_in_sb[64 * h:64 * h + 64, :], start=True, stop=True)
                    last.then_inc(mixed, 1)

            def pixels(img, j, q, c):
                pe.wait_ge(framed, reached(img.count(4 * STRIPS, 4 * j + 2 * q + 2)))
                pe.wait_ge(kept, reached(img.count(4 * STRIPS, 4 * j + 2 * q + c)))
                for t in range(4):
                    last = nc.tensor.matmul(fresh[:, t, :], filtered[:, j % 2, 4 * q + t, HID * c:HID * c + HID],
                                            to_pixels, start=True, stop=True)
                last.then_inc(fresh_full, 1)

            def start_taps(img, j, c):
                pe.wait_ge(haloed, reached(img.count(2 * STRIPS, 2 * j + (2 if j % STRIPS == STRIPS - 1 else 3))))
                if c == 0:
                    pe.wait_ge(gelu_done, reached(img.strip(j)))
                else:
                    pe.wait_ge(second_kept, reached(img.strip(j)))
                for q in range(2):
                    for n in range(PE_TAPS[c]):
                        last = nc.tensor.matmul(sums[c][:, 4 * q:4 * q + 4, :], diagonals[:, c, n, :],
                                                plane[:, j % RING, c, 4 * q + n // 3:4 * q + n // 3 + 4, n % 3:n % 3 + W],
                                                start=(n == 0), stop=(n == PE_TAPS[c] - 1))
                last.then_inc(started, 1)

            def side_bank(use):
                pe.wait_ge(side_free, reached(use - 1))

            def project(img, j):
                h = ((j - 4) % STRIPS) // STEPS
                side_bank(img.use(j, "P"))
                pe.wait_ge(gated, reached(img.strip(j - 3)))
                for q, part in enumerate((h, 1 - h)):
                    last = nc.tensor.matmul(side[64 * part:64 * part + 64, :], w_out_sb[:, :],
                                            gate[:, (j - 4) % 2, 512 * q:512 * q + 512], start=True, stop=True)
                last.then_inc(side_full, 1)

            def turn(img, j, d, k, i):
                side_bank(img.use(j, f"T{i}"))
                if i == 0:
                    pe.wait_ge(x1_done, reached(img.count(2 * STEPS, 2 * STEPS, d)))
                for t in range(4):
                    last = nc.tensor.transpose(side[:, 128 * t:128 * t + 128], X[(img.like + d) % 2][:, PS * k + 4 * i + t, :], ident)
                last.then_inc(side_full, 1)

            def spectrum(img, j, i):
                side_bank(img.use(j, f"D{i}"))
                pe.wait_ge(side_free, reached(img.use(j, f"T{i}")))
                for t in range(4):
                    last = nc.tensor.matmul(side[:, 128 * t:128 * t + 128], turned[:, t, :], to_spectrum,
                                            start=True, stop=True)
                last.then_inc(side_full, 1)

            def conv(img, j, d, k, i):
                side_bank(img.use(j, f"C{i}"))
                pe.wait_ge(signed, reached(img.count(STEPS + 2, min(k + 1, STEPS - 1) + 3, d)))
                row = PS * k + 4 * i
                for tap in range(TAPS):
                    dy, dx = tap // 3, tap % 3
                    last = nc.tensor.matmul(side[:, :], w_conv[:, tap, :], signs[:, row + dy:row + dy + 4, dx:dx + W],
                                            start=(tap == 0), stop=(tap == TAPS - 1))
                last.then_inc(side_full, 1)

            def group_mean(img, j, name, columns):
                side_bank(img.use(j, name))
                for n, col in enumerate(columns):
                    last = nc.tensor.matmul(side[:, 0:1], average, col, start=(n == 0), stop=(n == len(columns) - 1))
                last.then_inc(side_full, 1)

            def slot(img, j):
                parts = normal_parts(img, j)
                if img.has(j - 1):
                    pixels(img, j - 1, 0, 0)
                if "step" in parts:
                    turn(img, j, *parts["step"], 0)
                if "conv" in parts:
                    conv(img, j, *parts["conv"], 0)
                if img.has(j - 1):
                    pixels(img, j - 1, 0, 1)
                if "step" in parts:
                    spectrum(img, j, 0)
                if img.has(j - 3):
                    start_taps(img, j - 3, 1)
                if "mean" in parts:
                    pe.wait_ge(summed, reached(img.count(STEPS, STEPS, parts["mean"][0])))
                    group_mean(img, j, "M", [x_sums[:, k:k + 1] for k in range(STEPS)])
                if "spread" in parts:
                    pe.wait_ge(own_moments, reached(img.count(2, 1, parts["spread"][0])))
                    group_mean(img, j, "S0", [mean_var[:, 0:1]])
                if img.has(j - 4):
                    project(img, j)
                if img.has(j):
                    mix(img, j, 1)
                if "spread" in parts:
                    pe.wait_ge(own_moments, reached(img.count(2, 2, parts["spread"][0])))
                    group_mean(img, j, "S1", [stat[:, 2:3]])
                if "step" in parts:
                    turn(img, j, *parts["step"], 1)
                if img.has(j - 1):
                    pixels(img, j - 1, 1, 0)
                if img.has(j - 2):
                    start_taps(img, j - 2, 0)
                if "conv" in parts:
                    conv(img, j, *parts["conv"], 1)
                if "step" in parts:
                    spectrum(img, j, 1)
                if img.has(j - 1):
                    pixels(img, j - 1, 1, 1)
                if img.has(j + 1) and img.like >= 0:
                    mix(img, j + 1, 0)

            def before():
                pe.wait_ge(diagonals_done, sum(PE_TAPS))
                mix(Image(0, 0), 0, 0)

            over_images(pe, slot, before)

        @block.vector
        def _(dve):
            nc.vector.memset(w_conv[:], 0.0).then_inc(cleared, 1)
            nc.vector.memset(plane[:], 0.0).then_inc(cleared, 1)
            dve.wait_ge(weights_in, 16 * 9)
            for c in range(2):
                for n in range(PE_TAPS[c]):
                    nc.vector.tensor_scalar(diagonals[:, c, n, :], ident, w_dw_sb[:, c, n:n + 1], None,
                                            ALU.mult).then_inc(diagonals_done, 1)
            dve.wait_ge(tables_raw, 1)
            nc.vector.tensor_copy(gains[:, :], side[:, 0:256]).then_inc(tables, 1)

            def chunk_moments(Xa, k, i):
                return nc.vector.bn_stats(moments[:, 2 * k + i, :],
                                          Xa[:, PS * k + 4 * i:PS * k + 4 * i + 4, :].rearrange("p r w -> p (r w)"))

            def aggregate(img, j, d):
                dve.wait_ge(own, reached(img.count(2, 1, d)))
                nc.vector.memset(stat[:, 6:7], 0.0)
                nc.vector.bn_aggr(mean_var[:, :], moments[:, :, :].rearrange("p n s -> p (n s)")).then_inc(own_moments, 1)

            def mean_part(img, j, d):
                dve.wait_ge(side_full, reached(img.use(j, "M")))
                nc.vector.tensor_scalar(neg_mean[:, :], side[:, 0:1], -1.0 / (STEPS * CHUNK), None, ALU.mult).then_inc(centred, 1)
                dve.wait_ge(centred, reached(img.count(1, 1, d)))
                nc.vector.tensor_copy(stat[:, 4:5], side[:, 0:1]).then_inc(side_free, 1)

            def spread_part(img, j, d):
                dve.wait_ge(side_full, reached(img.use(j, "S0")))
                dve.wait_ge(own_moments, reached(img.count(2, 1, d)))
                nc.vector.tensor_scalar(stat[:, 0:1], side[:, 0:1], -float(PS), None, ALU.mult).then_inc(own, 1)
                nc.vector.tensor_tensor(stat[:, 1:2], side[:, 0:1], mean_var[:, 0:1], ALU.subtract).then_inc(side_free, 1)
                dve.wait_ge(side_free, reached(img.use(j, "S0")))
                nc.vector.scalar_tensor_tensor(out=stat[:, 2:3], in0=stat[:, 1:2], scalar=stat[:, 1:2],
                                               in1=mean_var[:, 1:2], op0=ALU.mult, op1=ALU.add).then_inc(own_moments, 1)

            def variance_part(img, j, d):
                dve.wait_ge(side_full, reached(img.use(j, "S1")))
                nc.vector.tensor_scalar(stat[:, 3:4], side[:, 0:1], EPS, None, ALU.add).then_inc(with_eps, 1)
                dve.wait_ge(with_eps, reached(img.count(1, 1, d)))
                nc.vector.tensor_copy(stat[:, 5:6], side[:, 0:1]).then_inc(side_free, 1)

            def conv_moments(img, d, k, i):
                dve.wait_ge(x1_done, reached(img.count(2 * STEPS, 2 * k + i + 1, d)))
                last = chunk_moments(X[(img.like + d) % 2], k, i)
                if (k, i) == (STEPS - 1, 1):
                    last.then_inc(own, 1)

            def add_taps(img, j, c, first, last):
                if first == 0:
                    dve.wait_ge(started, reached(img.count(2 * STRIPS, 2 * j + c + 1)))
                for n in range(first, last):
                    tap, q = PE_TAPS[c] + n // 2, n % 2
                    if n >= 2:
                        dve.wait_ge(tapped, reached(taps_done(img, j, c, n - 1)))
                    rows = sums[c][:, 4 * q:4 * q + 4, :]
                    nc.vector.scalar_tensor_tensor(
                        out=rows,
                        in0=plane[:, j % RING, c, 4 * q + tap // 3:4 * q + tap // 3 + 4, tap % 3:tap % 3 + W],
                        scalar=w_dw_sb[:, c, tap:tap + 1], in1=rows, op0=ALU.mult, op1=ALU.add).then_inc(tapped, 1)

            def slot(img, j):
                parts = normal_parts(img, j)

                def taps(c, half):
                    n = vector_taps(c)
                    if img.has(j - 3):
                        add_taps(img, j - 3, c, n * half, n * (half + 1))

                taps(0, 0)
                if "late" in parts and "spread" in parts:
                    conv_moments(img, *parts["late"], 1)
                if "spread" in parts:
                    aggregate(img, j, parts["spread"][0])
                taps(0, 1)
                if "late" in parts and "spread" not in parts:
                    conv_moments(img, *parts["late"], 1)
                if "mean" in parts:
                    mean_part(img, j, parts["mean"][0])
                if "spread" in parts:
                    spread_part(img, j, parts["spread"][0])
                taps(1, 0)
                if "spread" in parts:
                    variance_part(img, j, parts["spread"][0])
                taps(1, 1)
                if "conv" in parts:
                    conv_moments(img, *parts["conv"], 0)

            over_images(dve, slot)


def fourier_constants():
    import numpy as np
    y, x = np.meshgrid(np.arange(PS), np.arange(PS), indexing="ij")
    basis, pick = [], []
    for v in range(PS // 2 + 1):
        for u in range(PS):
            paired = v in (0, PS // 2)
            if paired and u > PS // 2:
                continue
            angle = 2 * np.pi * (u * y + v * x) / PS
            own = np.zeros((PS, PS // 2 + 1))
            if paired:
                own[u, v] += 0.5
                own[-u % PS, v] += 0.5
            else:
                own[u, v] = 1
            if paired and u in (0, PS // 2):
                members = [np.cos(angle) / PS]
            else:
                members = [f(angle) * np.sqrt(2) / PS for f in (np.cos, np.sin)]
            for q in members:
                basis.append(q.ravel())
                pick.append(own.ravel())
    basis, pick = np.stack(basis), np.stack(pick, 1)
    ident = np.eye(128)
    average = np.zeros((128, 128))
    for p in range(128):
        for o in range(128):
            if (p % C) // 2 == (o % C) // 2:
                average[p, o] = 0.25
    to_pixels = np.kron(np.eye(2), basis)
    square = np.stack([ident, average, to_pixels.T, to_pixels], 1)
    return {"square": square.astype(np.float32), "pick": np.concatenate([pick, pick], 1).astype(np.float32)}


def kernel(**inputs):
    import numpy as np
    import concourse.bacc as bacc
    from concourse.bass_utils import run_bass_kernel_spmd as run

    a = {k: np.asarray(v) for k, v in inputs.items()}
    arrays = {
        "x": a["x"],
        "w0": a["L0_conv_weight"].transpose(1, 2, 3, 0).reshape(C, TAPS, C),
        "w_in": a["L1_conv_w_in"].T,
        "w_dw": a["L1_conv_w_dw"].reshape(2 * HID, TAPS),
        "fft": a["L1_conv_fft_params"].reshape(2 * HID, 5 * PS).T,
        "w_out": a["L1_conv_w_out"].T,
    }
    arrays.update(fourier_constants())
    arrays = {k: np.ascontiguousarray(v) for k, v in arrays.items()}
    nc = bacc.Bacc("TRN2", target_bir_lowering=False, num_devices=1)
    args = [nc.dram_tensor(f"in_{k}", v.shape, mybir.dt.from_np(v.dtype), kind="ExternalInput").ap()
            for k, v in arrays.items()]
    out = nc.dram_tensor("result", a["x"].shape, F32, kind="ExternalOutput").ap()
    preact_layers(nc, *args, out)
    got = run(nc, [{f"in_{k}": v for k, v in arrays.items()}], core_ids=[0])
    return got.results[0]["result"]
```
